# Optimizing a Trainium2 kernel written in Bass

```python
import numpy as np
import jax
import jax.numpy as jnp

def _softmax(x, axis=-1):
    return jax.nn.softmax(x, axis=axis)

def _gelu(x):
    return jax.nn.gelu(x, approximate=True)

def _silu(x):
    return jax.nn.silu(x)

def _sigmoid(x):
    return jax.nn.sigmoid(x)

def _layernorm(x, axis=-1, eps=1e-05):
    m = jnp.mean(x, axis=axis, keepdims=True)
    v = jnp.var(x, axis=axis, keepdims=True)
    return (x - m) / jnp.sqrt(v + eps)

def _scatter_add(tgt, idx, src, axis=0):
    return tgt.at[idx].add(src)

def _segment_sum(src, seg, n):
    return jax.ops.segment_sum(src, seg, n)
kernel_name = 'mk_flamingo_gated_d1_seqx_r8_7691e2'

def setup_inputs(seed: int=0):
    np.random.seed(seed)
    _w = jnp.asarray

    def _rec_inputs():
        import jax
        import jax.numpy as jnp
        _rk = jax.random.key(seed)
        x = -0.0002928 + 1 * jax.random.normal(jax.random.fold_in(_rk, 1), (8, 56, 128), jnp.float32)
        _lenS = 56 - jax.random.randint(jax.random.fold_in(_rk, 7), (8,), 0, max(1, 56 // 4) + 1, jnp.int32)
        _lenS2 = 1500 - jax.random.randint(jax.random.fold_in(_rk, 8), (8,), 0, max(1, 1500 // 4) + 1, jnp.int32)
        _ctx_1024P = jax.random.normal(jax.random.fold_in(_rk, 11), (8, 16, 128), jnp.float32)
        _ctx_1024c = jax.random.dirichlet(jax.random.fold_in(_rk, 511), 0.3 * jnp.ones((16,), jnp.float32), (8, 1500))
        _ctx_1024t = jnp.einsum('bsk,bkd->bsd', _ctx_1024c, _ctx_1024P)
        _ctx_1024t = _ctx_1024t * jax.lax.rsqrt(jnp.mean(jnp.square(_ctx_1024t)) + 1e-12) * 0.953939
        ctx_1024 = 2.81802e-05 + 1.00001 * (_ctx_1024t + 0.3 * jax.random.normal(jax.random.fold_in(_rk, 611), (8, 1500, 128), jnp.float32))
        _g = jax.random.normal(jax.random.fold_in(_rk, 9001), (2, 1), jnp.float32)
        _g = jnp.sign(_g) * jnp.maximum(jnp.abs(_g), 1.0) + (_g == 0) * 1.0
        g_xattn = _g[0]
        g_ffn = _g[1]
        return (x, ctx_1024, g_xattn, g_ffn)
    x, ctx_1024, g_xattn, g_ffn = _rec_inputs()

    def _L0_xattn_setup():
        import jax, jax.numpy as jnp
        import numpy as np
        D_MODEL = 128
        N_HEADS = 16
        HEAD_DIM = D_MODEL // N_HEADS
        key = jax.random.key(seed)
        k1, k2, k3, k4, k5, k6 = jax.random.split(key, 6)
        B, T_q, T_kv = (4, 128, 512)
        s = 1.0 / np.sqrt(D_MODEL)
        return {'query': jax.random.normal(k1, (B, T_q, D_MODEL), dtype=jnp.float32), 'kv_source': jax.random.normal(k2, (B, T_kv, D_MODEL), dtype=jnp.float32), 'w_q': jax.random.normal(k3, (D_MODEL, D_MODEL), dtype=jnp.float32) * s, 'w_k': jax.random.normal(k4, (D_MODEL, D_MODEL), dtype=jnp.float32) * s, 'w_v': jax.random.normal(k5, (D_MODEL, D_MODEL), dtype=jnp.float32) * s, 'w_o': jax.random.normal(k6, (D_MODEL, D_MODEL), dtype=jnp.float32) * s}
    _L0_xattn_all = _L0_xattn_setup()
    _L0_xattn_in = {k: v for k, v in _L0_xattn_all.items() if k in ('w_q', 'w_k', 'w_v', 'w_o')}
    del _L0_xattn_all

    def _L0_ffn_setup():
        import jax, jax.numpy as jnp
        import numpy as np
        H = 128
        F = 512
        E = 8
        TOP_K = 2
        B, S = (1, 256)
        key = jax.random.key(seed)
        k0, k1, k2, k3 = jax.random.split(key, 4)
        hidden_states = jax.random.normal(k0, (B, S, H), dtype=jnp.float32)
        gate_w = jax.random.normal(k1, (E, H), dtype=jnp.float32) * 0.02
        gate_up_w = jax.random.normal(k2, (E, 2 * F, H), dtype=jnp.float32) * 0.02
        down_w = jax.random.normal(k3, (E, H, F), dtype=jnp.float32) * 0.02
        return {'hidden_states': hidden_states, 'gate_w': gate_w, 'gate_up_w': gate_up_w, 'down_w': down_w}
    _L0_ffn_all = _L0_ffn_setup()
    _L0_ffn_in = {k: v for k, v in _L0_ffn_all.items() if k in ('gate_w', 'gate_up_w', 'down_w')}
    del _L0_ffn_all
    return {'x': x, 'ctx_1024': ctx_1024, 'g_xattn': g_xattn, 'g_ffn': g_ffn, 'L0_xattn_w_q': _L0_xattn_in['w_q'], 'L0_xattn_w_k': _L0_xattn_in['w_k'], 'L0_xattn_w_v': _L0_xattn_in['w_v'], 'L0_xattn_w_o': _L0_xattn_in['w_o'], 'L0_ffn_gate_w': _L0_ffn_in['gate_w'], 'L0_ffn_gate_up_w': _L0_ffn_in['gate_up_w'], 'L0_ffn_down_w': _L0_ffn_in['down_w']}

def reference(x, ctx_1024, g_xattn, g_ffn, L0_xattn_w_q, L0_xattn_w_k, L0_xattn_w_v, L0_xattn_w_o, L0_ffn_gate_w, L0_ffn_gate_up_w, L0_ffn_down_w):
    import jax
    import jax.numpy as jnp

    def _L0_xattn_ref(query, kv_source, w_q, w_k, w_v, w_o):
        import jax, jax.numpy as jnp
        import numpy as np
        D_MODEL = 128
        N_HEADS = 16
        HEAD_DIM = D_MODEL // N_HEADS
        B, T_q, _ = query.shape
        T_kv = kv_source.shape[1]
        q = (query @ w_q.T).reshape(B, T_q, N_HEADS, HEAD_DIM)
        k = (kv_source @ w_k.T).reshape(B, T_kv, N_HEADS, HEAD_DIM)
        v = (kv_source @ w_v.T).reshape(B, T_kv, N_HEADS, HEAD_DIM)
        scale = HEAD_DIM ** (-0.5)
        attn = jax.nn.softmax(jnp.einsum('bqhd,bkhd->bhqk', q, k) * scale, axis=-1)
        out = jnp.einsum('bhqk,bkhd->bqhd', attn, v).reshape(B, T_q, D_MODEL)
        return out @ w_o.T

    def _L0_ffn_ref(hidden_states, gate_w, gate_up_w, down_w):
        import jax, jax.numpy as jnp
        import numpy as np
        H = 128
        F = 512
        E = 8
        TOP_K = 2
        B, S = (1, 256)
        b, s, h = hidden_states.shape
        x = hidden_states.reshape(-1, h)
        router_logits = x @ gate_w.T
        probs = jax.nn.softmax(router_logits.astype(jnp.float32), axis=-1)
        topw, sel = jax.lax.top_k(probs, TOP_K)
        topw = topw / jnp.sum(topw, axis=-1, keepdims=True)
        topw = topw.astype(x.dtype)
        combine = jnp.sum(jax.nn.one_hot(sel, E, dtype=x.dtype) * topw[..., None], axis=1)
        gu = jnp.einsum('th,efh->etf', x, gate_up_w)
        gate, up = (gu[..., :F], gu[..., F:])
        hact = up * jax.nn.gelu(gate, approximate=False)
        expert_out = jnp.einsum('etf,ehf->eth', hact, down_w)
        out = jnp.einsum('eth,te->th', expert_out, combine)
        return out.reshape(b, s, h)
    x = x + jnp.tanh(g_xattn[0]) * _L0_xattn_ref(_layernorm(x, axis=-1), ctx_1024, L0_xattn_w_q, L0_xattn_w_k, L0_xattn_w_v, L0_xattn_w_o)
    x = x + jnp.tanh(g_ffn[0]) * _L0_ffn_ref(_layernorm(x, axis=-1), L0_ffn_gate_w, L0_ffn_gate_up_w, L0_ffn_down_w)
    return x

_drawn_inputs = setup_inputs


def setup_inputs(seed=0):
    import zlib

    import numpy as np

    out = dict(_drawn_inputs(seed))
    spreads = {}
    factors = {'L0_ffn_gate_w': 8.0, 'L0_ffn_gate_up_w': 7.562, 'L0_ffn_down_w': 7.538}
    for name, (base, spread) in spreads.items():
        noise = np.random.default_rng([zlib.crc32(name.encode()), seed]).standard_normal(out[name].shape)
        drawn = base * np.exp(spread * noise) if base else spread * noise
        out[name] = jnp.asarray(drawn.astype(out[name].dtype))
    for name, factor in factors.items():
        out[name] = (out[name] * factor).astype(out[name].dtype)
    return out
```

```python
from contextlib import ExitStack

import concourse.bass as bass
from concourse import mybir

B, TQ, D = 8, 56, 128
TK = 1500
H, HD = 16, 8
E, F = 8, 512
EPS = 1e-5
SCALE = HD ** -0.5

TOK = B * TQ
NR = 4
RT = TOK // NR
KT = -(-TK // 128)
LAST = TK - 128 * (KT - 1)
KPAD = 128 * KT
NCH = 3
CK = 512
HT = 8
HALF = [(0, 128 * HT), (128 * HT, TK - 128 * HT)]
G, GC = 4, 4 * TQ
NP, PC = 8, 2 * TQ
SC = H * TQ
VP = 17
VW = VP * (NP - 1) + 32
MR = 96
KR = 112
MOVES = 16 * 12
MN = NCH * NP
FT = F // 128


def chunk(n):
    return CK * n, min(CK, TK - CK * n)


def max_product(n):
    return (n // 2, n % 2) if n < 2 * NP else (n - 2 * NP, 2)


def part_of(n):
    return {0: 0, 2 * NP: 1}.get(n)


def flamingo_block(nc, x, ctxT, g_attn, g_ffn, wqT, wkT, wvT, woT, gwT, guT, dnT, out):
    f32, f32r = mybir.dt.float32, mybir.dt.float32r
    ALU, ACT, AX = mybir.AluOpType, mybir.ActivationFunctionType, mybir.AxisListType

    with ExitStack() as stack:
        def sb(name, shape, dt=f32):
            return stack.enter_context(nc.sbuf_tensor(name, shape, dt))

        def pb(name, shape):
            return stack.enter_context(nc.psum_tensor(name, shape, f32))

        def sem(name):
            return stack.enter_context(nc.semaphore(name))

        kx = sb("kx", [128, 2, G, KPAD], f32r)
        qx = sb("qx", [128, 2, G, GC], f32r)
        qx_all = sb("qx_all", [MR, B, SC])
        k_high = sb("k_high", [128, KPAD], f32r)
        k_low = sb("k_low", [128, KPAD], f32r)
        ctx_sb = sb("ctx_sb", [128, 2, KPAD])
        v_sb = sb("v_sb", [128, 2, KT, VW])
        probs = sb("probs", [128, 2, SC])
        o_sb = sb("o_sb", [128, 2 * PC])
        o_norm = sb("o_norm", [128, NR, 4, 2, TQ])
        inv_den = sb("inv_den", [128, 2 * PC])
        part_max = sb("part_max", [PC, NP, NCH])
        neg_max = sb("neg_max", [PC, NP])
        neg_max_parts = sb("neg_max_parts", [PC, 2, NP], f32r)
        wq_sb, wk_sb, wv_sb = sb("wq_sb", [D, D]), sb("wk_sb", [D, D]), sb("wv_sb", [D, D])
        wo_sb = sb("wo_sb", [128, 4, D])
        gw_sb = sb("gw_sb", [D, E])
        gu_sb = sb("gu_sb", [D, E, 2 * F])
        dn_sb = sb("dn_sb", [128, E, FT, D])
        x_sb = sb("x_sb", [RT, NR, D])
        xn = sb("xn", [RT, NR, D])
        xnT = sb("xnT", [D, TOK])
        q_high = sb("q_high", [D, TOK], f32r)
        q_low = sb("q_low", [D, TOK], f32r)
        x1 = sb("x1", [RT, NR, D])
        stats = sb("stats", [RT, NR, 6])
        mean_var = sb("mean_var", [RT, NR, 2])
        var_eps = sb("var_eps", [RT, NR])
        rstd = sb("rstd", [RT, NR])
        minus_half = sb("minus_half", [RT, NR])
        gates = sb("gates", [128, 2])
        tanh_g = sb("tanh_g", [128, 2])
        ident = sb("ident", [128, 128])
        head_mask3 = sb("head_mask3", [128, G, 4])
        head_mask = sb("head_mask", [128, 4])
        den_sel = sb("den_sel", [128, 128])
        row_mask = sb("row_mask", [16, NP])
        expert_sel = sb("expert_sel", [16, E, 128], f32r)
        before = sb("before", [RT, E, E])
        logits = sb("logits", [RT, NR, E])
        row8 = sb("row8", [RT, 4, NR])
        pr = sb("pr", [RT, NR, E])
        rank = sb("rank", [RT, NR, E])
        comb = sb("comb", [RT, NR, E])
        comb_parts = sb("comb_parts", [RT, NR, 2, E], f32r)
        combT = q_high[0:16, :]
        out_sb = xn
        qd_high = probs[:, :, :].rearrange("p a c -> p (a c)")
        qd_low = o_norm[:, :, :, :, :].rearrange("p r s b c -> p (r s b c)")
        greater = ctx_sb[0:RT, 0, 0:NR * E * E].rearrange("t (r e j) -> t r e j", r=NR, e=E)
        equal = ctx_sb[0:RT, 1, 0:NR * E * E].rearrange("t (r e j) -> t r e j", r=NR, e=E)
        gelu_sb = probs[:, 0, :].rearrange("p (a t) -> p a t", a=2)
        hact = probs[:, 1, :].rearrange("p (a t) -> p a t", a=2)
        x_expert = qd_low[:, 0:2 * TOK].rearrange("p (a t) -> p a t", a=2)
        yT = qd_low[:, 2 * TOK:3 * TOK]

        score_ps = pb("score_ps", [128, 2, 2, 512])
        max_ps = pb("max_ps", [128, 2, 512])
        o_ps = pb("o_ps", [128, 512])
        misc_ps = pb("misc_ps", [128, 512])

        x_loaded, w_loaded, wo_loaded, ffn_loaded, g_loaded = map(sem, ("x_loaded", "w_loaded", "wo_loaded", "ffn_loaded", "g_loaded"))
        ctx_loaded = [sem("ctx_loaded0"), sem("ctx_loaded1")]
        kx_loaded = [[sem(f"kx_loaded{p}{h}") for h in range(2)] for p in range(2)]
        qx_moved = sem("qx_moved")
        consts, cleared, wo_cleared, pool_step = map(sem, ("consts", "cleared", "wo_cleared", "pool_step"))
        var_ready, rstd_ready, xn_ready, xT_done, xT_saved = map(sem, ("var_ready", "rstd_ready", "xn_ready", "xT_done", "xT_saved"))
        q_done, q_high_saved, q_low_saved, qd_ready = map(sem, ("q_done", "q_high_saved", "q_low_saved", "qd_ready"))
        k_done, k_high_saved, k_low_saved = map(sem, ("k_done", "k_high_saved", "k_low_saved"))
        v_done, v_saved = map(sem, ("v_done", "v_saved"))
        kx_ones, qx_ready = sem("kx_ones"), sem("qx_ready")
        scores_done, exp_done, pv_done = map(sem, ("scores_done", "exp_done", "pv_done"))
        max_done, max_taken = map(sem, ("max_done", "max_taken"))
        nm_step, nmT_done, nm_rows = map(sem, ("nm_step", "nmT_done", "nm_rows"))
        o_saved, den_done, den_taken, o_norm_ready = map(sem, ("o_saved", "den_done", "den_taken", "o_norm_ready"))
        ln_step, tanh_ready = map(sem, ("ln_step", "tanh_ready"))
        wo_done, x1_ready = map(sem, ("wo_done", "x1_ready"))
        logits_done, logits_exp, router_step, comb_ready = map(sem, ("logits_done", "logits_exp", "router_step", "comb_ready"))
        combT_done, combT_saved = map(sem, ("combT_done", "combT_saved"))
        bc_done, xe_ready = map(sem, ("bc_done", "xe_ready"))
        gate_done, up_done, gelu_ready, hact_ready, down_done = map(sem, ("gate_done", "up_done", "gelu_ready", "hact_ready", "down_done"))
        y_saved, yT_done, out_ready, stored = map(sem, ("y_saved", "yT_done", "out_ready", "stored"))

        block = stack.enter_context(nc.Block())

        def bc(ap, shape):
            return ap.to_broadcast(shape)

        def nxt(i, par, k):
            return i + (par + k) // 2, (par + k) % 2

        def batch(i, par):
            return 2 * i + par

        def counts(eng, *values):
            for v in values:
                if not isinstance(v, int):
                    eng.lower_val(v)
            return values

        @block.sync
        def _(sp):
            def move_keys(i, par, half):
                start, size = HALF[half]
                for row, part in ((0, k_high), (1, k_low), (2, k_high)):
                    for g in range(G):
                        sp.dma_start(kx[32 * row:32 * row + 32, par, g, start:start + size].bitcast(f32),
                                     part[32 * g:32 * g + 32, start:start + size].bitcast(f32)
                                     ).then_inc(kx_loaded[par][half], 16)

            sp.dma_start(x_sb[:, :, :], x).then_inc(x_loaded, 16)
            sp.dma_start(wk_sb[:, :], wkT).then_inc(w_loaded, 16)
            sp.dma_start(ctx_sb[:, 0, 0:TK], ctxT[0]).then_inc(ctx_loaded[0], 16)
            sp.dma_start(ctx_sb[:, 1, 0:TK], ctxT[1]).then_inc(ctx_loaded[1], 16)
            for half in range(2):
                sp.wait_ge(k_low_saved, 2 + half)
                move_keys(0, 0, half)
            sp.wait_ge(k_low_saved, NCH + 2)
            move_keys(0, 1, 0)
            sp.wait_ge(v_done, 3)
            sp.dma_start(ctx_sb[:, 0, 0:TK], ctxT[2]).then_inc(ctx_loaded[0], 16)

            def body(i, par, ctx_next=True, keys_next=True):
                b = batch(i, par)
                i1, par1 = nxt(i, par, 1)
                split_2, split_1, left_2, left_1, taken = counts(
                    sp, NCH * (b + 2), NCH * (b + 2) + 2, KT * b + 1, KT * b + HT, 3 * (b + 2))
                sp.wait_ge(k_low_saved, split_2)
                sp.wait_ge(scores_done, left_2)
                move_keys(i1, par1, 1)
                if keys_next:
                    sp.wait_ge(k_low_saved, split_1)
                    sp.wait_ge(scores_done, left_1)
                    move_keys(i + 1, par, 0)
                if ctx_next:
                    sp.wait_ge(v_done, taken)
                    sp.dma_start(ctx_sb[:, par1, 0:TK], ctxT[b + 3]).then_inc(ctx_loaded[par1], 16)

            with sp.Fori(0, 2) as i:
                body(i, 0)
                body(i, 1)
            body(2, 0)
            body(2, 1, ctx_next=False)
            body(3, 0, ctx_next=False, keys_next=False)
            sp.wait_ge(out_ready, NR)
            sp.dma_start(out, out_sb[:, :, :]).then_inc(stored, 16)
            sp.wait_ge(stored, 16)

        @block.gpsimd
        def _(pool):
            steps = [0]

            def serial(ins):
                steps[0] += 1
                ins.then_inc(pool_step, 1)
                pool.wait_ge(pool_step, steps[0])

            serial(nc.gpsimd.memset(minus_half[:, :], -0.5))
            serial(nc.gpsimd.memset(ident[:, :], 0.0))
            serial(nc.gpsimd.affine_select(out=ident[:, :], in_=ident[:, :], compare_op=ALU.not_equal, fill=1.0,
                                           base=0, pattern=[[-1, 128]], channel_multiplier=1))
            serial(nc.gpsimd.memset(head_mask3[:, :, :], 1.0))
            serial(nc.gpsimd.affine_select(out=head_mask3[:, :, :], in_=head_mask3[:, :, :], compare_op=ALU.is_ge,
                                           fill=0.0, base=0, pattern=[[-32, G], [-HD, 4]], channel_multiplier=1))
            serial(nc.gpsimd.affine_select(out=head_mask3[:, :, :], in_=head_mask3[:, :, :], compare_op=ALU.is_ge,
                                           fill=0.0, base=HD - 1, pattern=[[32, G], [HD, 4]], channel_multiplier=-1))
            serial(nc.gpsimd.memset(row_mask[:, :], 0.0))
            for r in (0, NP):
                serial(nc.gpsimd.affine_select(out=row_mask[:, :], in_=row_mask[:, :], compare_op=ALU.not_equal,
                                               fill=1.0, base=-r, pattern=[[-1, NP]], channel_multiplier=1))
            serial(nc.gpsimd.memset(den_sel[:, :], 0.0))
            sel = den_sel[:, :].rearrange("k (j m) -> k j m", j=4)
            serial(nc.gpsimd.affine_select(out=sel, in_=sel, compare_op=ALU.not_equal, fill=1.0,
                                           base=-16, pattern=[[-32, 4], [0, 32]], channel_multiplier=1))
            serial(nc.gpsimd.memset(before[:, :, :], 1.0))
            nc.gpsimd.affine_select(out=before[:, :, :], in_=before[:, :, :], compare_op=ALU.is_ge, fill=0.0,
                                    base=-1, pattern=[[1, E], [-1, E]], channel_multiplier=0).then_inc(consts, 1)
            pool.wait_ge(consts, 1)
            pool.wait_ge(var_ready, 1)
            nc.gpsimd.tensor_tensor(rstd[:, :], var_eps[:, :], minus_half[:, :], ALU.pow).then_inc(rstd_ready, 1)

            pool.wait_ge(wo_cleared, 1)
            for s in range(2):
                for i in range(2):
                    for j in range(4):
                        h = 2 * (4 * s + j) + i
                        r = 32 * j + HD * i
                        pool.dma_start(wo_sb[r:r + HD, 2 * s + i, :], woT[HD * h:HD * h + HD, :]).then_inc(wo_loaded, 16)

            def stage(b, par):
                nc.gpsimd.tensor_copy(qx[0:MR, par, :, :],
                                      qx_all[:, b, :].rearrange("p (g c) -> p g c", g=G)).then_inc(qx_ready, 1)

            pool.wait_ge(rstd_ready, 1)
            nc.gpsimd.memset(kx[MR:128, :, :, :].bitcast(f32), 1.0).then_inc(kx_ones, 1)
            pool.wait_ge(kx_ones, 1)
            pool.wait_ge(qx_moved, MOVES)
            stage(0, 0)
            pool.wait_ge(qx_ready, 1)
            stage(1, 1)

            def body(i, par):
                b = batch(i, par)
                staged, left = counts(pool, b + 2, KT * (b + 1))
                pool.wait_ge(qx_ready, staged)
                pool.wait_ge(scores_done, left)
                stage(b + 2, par)

            with pool.Fori(0, B // 2 - 1) as i:
                body(i, 0)
                body(i, 1)
            pool.wait_ge(qx_ready, B)
            pool.wait_ge(var_ready, 2)
            nc.gpsimd.tensor_tensor(rstd[:, :], var_eps[:, :], minus_half[:, :], ALU.pow).then_inc(rstd_ready, 1)

        @block.scalar
        def _(act):
            act.dma_start(wq_sb[:, :], wqT).then_inc(w_loaded, 16)
            act.dma_start(wv_sb[:, :], wvT).then_inc(w_loaded, 16)
            act.dma_start(gates[:, 0:1], g_attn.partition_broadcast(128)).then_inc(g_loaded, 16)
            act.dma_start(gates[:, 1:2], g_ffn.partition_broadcast(128)).then_inc(g_loaded, 16)
            act.wait_ge(g_loaded, 32)
            nc.scalar.activation(tanh_g[:, :], gates[:, :], ACT.Tanh).then_inc(tanh_ready, 1)

            def k_copy(b, n, bank, moved=None, move_count=0):
                start, size = chunk(n)
                projected, move_count = counts(act, NCH * b + n + 1, move_count)
                if moved is not None:
                    act.wait_ge(moved, move_count)
                act.wait_ge(k_done, projected)
                nc.scalar.activation(k_high[:, start:start + size], bank[:, 0:size], ACT.Copy).then_inc(k_high_saved, 1)

            def v_copy(b, par, n):
                act.wait_ge(v_done, 3 * b + n + 1)
                dst = v_sb[:, par, 4 * n:4 * n + 4, 0:VP * NP].rearrange("k t (p c) -> k t p c", p=NP)[:, :, :, 0:16]
                src = misc_ps[:, :].rearrange("k (t p c) -> k t p c", t=4, p=NP)
                nc.scalar.activation(dst, src, ACT.Copy).then_inc(v_saved, 1)

            def exp_tile(b, t):
                act.wait_ge(scores_done, KT * b + t + 1)
                m = 128 if t < KT - 1 else LAST
                nc.scalar.activation(probs[0:m, t % 2, :].rearrange("k (a c) -> k a c", a=2),
                                     score_ps[0:m, t % 2, :, 0:SC // 2], ACT.Exp, scale=SCALE).then_inc(exp_done, 1)

            for n in range(NCH):
                k_copy(0, n, score_ps[:, n // 2, n % 2, :])
            act.wait_ge(xT_done, 1)
            nc.scalar.activation(xnT[:, :], misc_ps[:, 0:TOK], ACT.Copy).then_inc(xT_saved, 1)
            act.wait_ge(q_done, 1)
            nc.scalar.activation(q_high[:, :], max_ps[:, 0, 0:TOK], ACT.Copy).then_inc(q_high_saved, 1)
            act.wait_ge(qd_ready, 2)
            for row, part in ((0, qd_high), (1, qd_high), (2, qd_low)):
                for g in range(G):
                    src = part[32 * g:32 * g + 32, :].rearrange("p (b c) -> p b c", b=B)
                    act.dma_start(qx_all[32 * row:32 * row + 32, :, GC * g:GC * g + GC], src).then_inc(qx_moved, 16)
            act.dma_start(gw_sb[:, :], gwT).then_inc(ffn_loaded, 16)
            act.dma_start(gu_sb[:, :, :], guT).then_inc(ffn_loaded, 16)
            act.dma_start(dn_sb[:, :, :, :], dnT).then_inc(ffn_loaded, 16)
            for n in range(NCH):
                k_copy(1, n, score_ps[:, n // 2, n % 2, :], kx_loaded[0][n // 2] if n != 1 else None, MOVES)
            act.wait_ge(cleared, 1)
            for n in range(3):
                v_copy(0, 0, n)
            act.wait_ge(qx_moved, MOVES)
            exp_tile(0, 0)

            def body(i, par, keys_next=True, next_batch=True):
                b = batch(i, par)
                i1, par1 = nxt(i, par, 1)
                for t in range(KT):
                    if t < KT - 1:
                        exp_tile(b, t + 1)
                    elif next_batch:
                        exp_tile(b + 1, 0)
                    if next_batch and t in V_STEPS:
                        v_copy(b + 1, par1, V_STEPS.index(t))
                    if keys_next and t in K_STEPS:
                        n = K_STEPS.index(t)
                        moved = kx_loaded[par1][n // 2] if n != 1 else None
                        k_copy(b + 2, n, misc_ps, moved, MOVES * (i1 + 1))

            with act.Fori(0, B // 2 - 1) as i:
                body(i, 0)
                body(i, 1)
            body(3, 0, keys_next=False)
            body(3, 1, keys_next=False, next_batch=False)

            act.wait_ge(xT_done, 2)
            nc.scalar.activation(xnT[:, :], misc_ps[:, 0:TOK], ACT.Copy).then_inc(xT_saved, 1)
            act.wait_ge(router_step, 2)
            nc.scalar.activation(pr[:, :, :], logits[:, :, :], ACT.Exp).then_inc(logits_exp, 1)
            act.wait_ge(combT_done, 1)
            nc.scalar.activation(combT, max_ps[0:16, 1, 0:TOK], ACT.Copy).then_inc(combT_saved, 1)
            for n in range(E * FT):
                act.wait_ge(gate_done, n + 1)
                if n >= 2:
                    act.wait_ge(hact_ready, n - 1)
                nc.scalar.activation(gelu_sb[:, n % 2, :], score_ps[:, n % 2, 0, 0:TOK], ACT.Gelu).then_inc(gelu_ready, 1)
            act.wait_ge(down_done, E * FT)
            nc.scalar.activation(yT, o_ps[:, 0:TOK], ACT.Copy).then_inc(y_saved, 1)

        @block.vector
        def _(dve):
            nc.vector.memset(wo_sb[:, :, :], 0.0).then_inc(wo_cleared, 1)
            ln = [0]

            def layer_norm(src, turn):
                for r in range(NR):
                    nc.vector.bn_stats(stats[:, r, :], src[:, r, :]).then_inc(ln_step, 1)
                    ln[0] += 1
                dve.wait_ge(ln_step, ln[0])
                for r in range(NR):
                    nc.vector.bn_aggr(mean_var[:, r, :], stats[:, r, :]).then_inc(ln_step, 1)
                    ln[0] += 1
                dve.wait_ge(ln_step, ln[0])
                nc.vector.tensor_scalar(var_eps[:, :], mean_var[:, :, 1], EPS, None, ALU.add).then_inc(var_ready, 1)
                dve.wait_ge(rstd_ready, turn)
                for r in range(NR):
                    nc.vector.tensor_scalar(xn[:, r, :], src[:, r, :], mean_var[:, r, 0:1], rstd[:, r:r + 1],
                                            ALU.subtract, ALU.mult).then_inc(xn_ready, 1)

            def k_rest(b, n, bank, moved=None, move_count=0):
                start, size = chunk(n)
                high, move_count = counts(dve, NCH * b + n + 1, move_count)
                if moved is not None:
                    dve.wait_ge(moved, move_count)
                dve.wait_ge(k_high_saved, high)
                nc.vector.tensor_tensor(k_low[:, start:start + size], bank[:, 0:size],
                                        k_high[:, start:start + size].bitcast(f32), ALU.subtract
                                        ).then_inc(k_low_saved, 1)

            def take_max(b, n):
                p, c = max_product(n)
                size = chunk(c)[1]
                dve.wait_ge(max_done, MN * b + n + 1)
                nc.vector.reduce_max(part_max[:, p, c:c + 1], max_ps[0:PC, n % 2, 0:size],
                                     AX.X).then_inc(max_taken, 1)

            def negate_max(b):
                dve.wait_ge(max_taken, MN * (b + 1))
                nc.vector.tensor_reduce(neg_max[:, :], part_max[:, :, :], AX.X, ALU.max, negate=True).then_inc(nm_step, 1)
                dve.wait_ge(nm_step, 3 * b + 1)
                nc.vector.tensor_copy(neg_max_parts[:, 0, :], neg_max[:, :]).then_inc(nm_step, 1)
                dve.wait_ge(nm_step, 3 * b + 2)
                nc.vector.tensor_tensor(neg_max_parts[:, 1, :], neg_max[:, :], neg_max_parts[:, 0, :].bitcast(f32),
                                        ALU.subtract).then_inc(nm_step, 1)

            def max_rows(b, par):
                dve.wait_ge(nmT_done, b + 1)
                dst = qx[MR:KR, par, :, :].rearrange("r g (p c) -> r (g p) c", p=2)
                nc.vector.tensor_tensor(dst, bc(misc_ps[0:16, 0:PC].unsqueeze(1), [16, NP, PC]),
                                        bc(row_mask[:, :].unsqueeze(2), [16, NP, PC]), ALU.mult).then_inc(nm_rows, 1)

            nc.vector.memset(ctx_sb[:, 0, TK:KPAD], 0.0).then_inc(o_norm_ready, 1)
            nc.vector.memset(ctx_sb[:, 1, TK:KPAD], 0.0).then_inc(den_taken, 1)
            dve.wait_ge(x_loaded, 16)
            layer_norm(x_sb, 1)
            for n in range(NCH):
                k_rest(0, n, score_ps[:, n // 2, n % 2, :])
            nc.vector.memset(v_sb[:, :, :, :], 1.0).then_inc(cleared, 1)
            dve.wait_ge(consts, 1)
            nc.vector.tensor_reduce(head_mask[:, :], head_mask3[:, :, :].rearrange("p g h -> p h g"), AX.X,
                                    ALU.add).then_inc(ln_step, 1)
            ln[0] += 1
            nc.vector.tensor_copy(expert_sel[:, :, :], bc(row_mask[:, :].unsqueeze(2), [16, E, 128]))
            dve.wait_ge(q_high_saved, 1)
            nc.vector.tensor_tensor(q_low[:, :], max_ps[:, 0, 0:TOK], q_high[:, :].bitcast(f32),
                                    ALU.subtract).then_inc(q_low_saved, 1)
            dve.wait_ge(ln_step, ln[0])
            dve.wait_ge(q_low_saved, 1)
            for part, dst in ((q_high, qd_high), (q_low, qd_low)):
                dst = dst.rearrange("p (b h c) -> p b h c", b=B, h=4)
                src = part[:, :].bitcast(f32).rearrange("p (b c) -> p b c", b=B).unsqueeze(2)
                mask = head_mask[:, :].unsqueeze(1).unsqueeze(3)
                nc.vector.tensor_tensor(dst, bc(src, [128, B, 4, TQ]), bc(mask, [128, B, 4, TQ]),
                                        ALU.mult).then_inc(qd_ready, 1)
            for n in range(NCH):
                k_rest(1, n, score_ps[:, n // 2, n % 2, :], kx_loaded[0][n // 2] if n != 1 else None, MOVES)
            for n in range(MN):
                take_max(0, n)
            negate_max(0)
            max_rows(0, 0)

            def body(i, par, keys_next=True, next_batch=True):
                b = batch(i, par)
                i1, par1 = nxt(i, par, 1)
                for t in range(KT):
                    for n in (MAX_STEPS[t] if next_batch else ()):
                        take_max(b + 1, n)
                    if next_batch and t == NM_STEP - 1:
                        negate_max(b + 1)
                    if next_batch and t == NM_STEP:
                        max_rows(b + 1, par1)
                    if t == KT - 1:
                        complete, normalised = counts(dve, b + 1, b + 1)
                        dve.wait_ge(o_norm_ready, normalised)
                        dve.wait_ge(pv_done, complete)
                        nc.vector.tensor_copy(o_sb[:, :], o_ps[:, 0:2 * PC]).then_inc(o_saved, 1)
                    if keys_next and t in K_STEPS:
                        n = K_STEPS.index(t)
                        moved = kx_loaded[par1][n // 2] if n != 1 else None
                        k_rest(b + 2, n, misc_ps, moved, MOVES * (i1 + 1))
                dve.wait_ge(den_done, b + 1)
                nc.vector.reciprocal(inv_den[:, :], max_ps[:, 1, 0:2 * PC]).then_inc(den_taken, 1)
                dve.wait_ge(den_taken, b + 2)
                four = "p (s c) -> p s c"
                nc.vector.tensor_tensor(o_norm[:, i, :, par, :], o_sb[:, :].rearrange(four, s=4),
                                        inv_den[:, :].rearrange(four, s=4), ALU.mult).then_inc(o_norm_ready, 1)

            with dve.Fori(0, B // 2 - 1) as i:
                body(i, 0)
                body(i, 1)
            body(3, 0, keys_next=False)
            body(3, 1, keys_next=False, next_batch=False)

            dve.wait_ge(tanh_ready, 1)
            for r in range(NR):
                dve.wait_ge(wo_done, r + 1)
                nc.vector.scalar_tensor_tensor(x1[:, r, :], score_ps[0:RT, r // 2, r % 2, 0:D], tanh_g[0:RT, 0:1],
                                               x_sb[:, r, :], ALU.mult, ALU.add).then_inc(x1_ready, 1)
            dve.wait_ge(x1_ready, NR)
            layer_norm(x1, 2)

            steps = [0]

            def serial(ins):
                steps[0] += 1
                ins.then_inc(router_step, 1)
                dve.wait_ge(router_step, steps[0])

            dve.wait_ge(logits_done, NR)
            raw = max_ps[0:RT, 0, 0:NR * E].rearrange("t (r e) -> t r e", r=NR)
            big = [RT, NR, E]
            serial(nc.vector.reduce_max(row8[:, 0, :], raw, AX.X))
            serial(nc.vector.tensor_tensor(logits[:, :, :], raw, bc(row8[:, 0, :].unsqueeze(2), big), ALU.subtract))
            dve.wait_ge(logits_exp, 1)
            serial(nc.vector.tensor_reduce(row8[:, 1, :], pr[:, :, :], AX.X, ALU.add))
            serial(nc.vector.reciprocal(row8[:, 2, :], row8[:, 1, :]))
            serial(nc.vector.tensor_tensor(pr[:, :, :], pr[:, :, :], bc(row8[:, 2, :].unsqueeze(2), big), ALU.mult))
            cube = [RT, NR, E, E]
            other, own = bc(pr[:, :, :].unsqueeze(2), cube), bc(pr[:, :, :].unsqueeze(3), cube)
            serial(nc.vector.tensor_tensor(equal, other, own, ALU.is_equal))
            serial(nc.vector.tensor_tensor(greater, other, own, ALU.is_gt))
            serial(nc.vector.tensor_tensor(equal, equal, bc(before[:, :, :].unsqueeze(1), cube),
                                           ALU.mult))
            serial(nc.vector.tensor_tensor(greater, greater, equal, ALU.add))
            serial(nc.vector.tensor_reduce(rank[:, :, :], greater, AX.X, ALU.add))
            serial(nc.vector.scalar_tensor_tensor(comb[:, :, :], rank[:, :, :], 1.5, pr[:, :, :], ALU.is_lt, ALU.mult))
            serial(nc.vector.tensor_reduce(row8[:, 3, :], comb[:, :, :], AX.X, ALU.add))
            serial(nc.vector.reciprocal(row8[:, 1, :], row8[:, 3, :]))
            serial(nc.vector.tensor_tensor(comb[:, :, :], comb[:, :, :], bc(row8[:, 1, :].unsqueeze(2), big), ALU.mult))
            serial(nc.vector.tensor_copy(comb_parts[:, :, 0, :], comb[:, :, :]))
            nc.vector.tensor_tensor(comb_parts[:, :, 1, :], comb[:, :, :], comb_parts[:, :, 0, :].bitcast(f32),
                                    ALU.subtract).then_inc(comb_ready, 1)

            dve.wait_ge(xT_saved, 2)

            def scale_tokens(e):
                dve.wait_ge(bc_done, e + 1)
                nc.vector.tensor_tensor(x_expert[:, e % 2, :], max_ps[:, e % 2, 0:TOK], xnT[:, :], ALU.mult
                                        ).then_inc(xe_ready, 1)

            scale_tokens(0)
            for n in range(E * FT):
                if n % FT == 0 and n // FT + 1 < E:
                    scale_tokens(n // FT + 1)
                dve.wait_ge(gelu_ready, n + 1)
                dve.wait_ge(up_done, n + 1)
                if n >= 2:
                    dve.wait_ge(down_done, n - 1)
                nc.vector.tensor_tensor(hact[:, n % 2, :], score_ps[:, n % 2, 1, 0:TOK], gelu_sb[:, n % 2, :],
                                        ALU.mult).then_inc(hact_ready, 1)
            for r in range(NR):
                dve.wait_ge(yT_done, r + 1)
                nc.vector.scalar_tensor_tensor(out_sb[:, r, :], score_ps[0:RT, r // 2, r % 2, 0:D], tanh_g[0:RT, 1:2],
                                               x1[:, r, :], ALU.mult, ALU.add).then_inc(out_ready, 1)

        @block.tensor
        def _(pe):
            def k_project(b, par, n, bank):
                start, size = chunk(n)
                nc.tensor.matmul(bank[:, 0:size], wk_sb[:, :], ctx_sb[:, par, start:start + size],
                                 start=True, stop=True).then_inc(k_done, 1)

            def v_project(par, n):
                for k in range(4):
                    t = 4 * n + k
                    last = nc.tensor.matmul(misc_ps[:, 128 * k:128 * k + 128], ctx_sb[:, par, 128 * t:128 * t + 128],
                                            wv_sb[:, :], start=True, stop=True)
                last.then_inc(v_done, 1)

            def scores(par, t, g0):
                m = 128 if t < KT - 1 else LAST
                for g in (g0, g0 + 1):
                    last = nc.tensor.matmul(score_ps[0:m, t % 2, g // 2, GC * (g % 2):GC * (g % 2) + GC],
                                            kx[0:KR, par, g, 128 * t:128 * t + m], qx[0:KR, par, g, :],
                                            start=True, stop=True)
                if g0 == 2:
                    last.then_inc(scores_done, 1)

            def max_scores(b, par, n):
                p, c = max_product(n)
                start, size = chunk(c)
                if n >= 2 or not (isinstance(b, int) and b == 0):
                    pe.wait_ge(max_taken, MN * b + n - 1)
                nc.tensor.matmul(max_ps[0:PC, n % 2, 0:size], qx[0:MR, par, p // 2, PC * (p % 2):PC * (p % 2) + PC],
                                 kx[0:MR, par, p // 2, start:start + size], start=True, stop=True
                                 ).then_inc(max_done, 1)

            def attend(par, t, s):
                m = 128 if t < KT - 1 else LAST
                for j in range(4):
                    p = 4 * s + j
                    last = nc.tensor.matmul(o_ps[32 * j:32 * j + 32, PC * s:PC * s + PC],
                                            v_sb[0:m, par, t, VP * p:VP * p + 32],
                                            probs[0:m, t % 2, PC * p:PC * p + PC],
                                            start=(t == 0 and s == 0), stop=(t == KT - 1), skip_group_check=True)
                return last

            def transpose_max(ready):
                pe.wait_ge(nm_step, ready)
                nc.tensor.matmul(misc_ps[0:16, 0:PC], neg_max_parts[:, :, :].bitcast(f32).rearrange("t a p -> t (a p)"),
                                 ident[0:PC, 0:PC], start=True, stop=True).then_inc(nmT_done, 1)

            pe.wait_ge(w_loaded, 48)
            pe.wait_ge(ctx_loaded[0], 16)
            for n in range(NCH):
                k_project(0, 0, n, score_ps[:, n // 2, n % 2, :])
            pe.wait_ge(consts, 1)
            for r in range(NR):
                pe.wait_ge(xn_ready, r + 1)
                last = nc.tensor.matmul(misc_ps[:, RT * r:RT * r + RT], xn[:, r, :], ident[0:RT, 0:RT],
                                        start=True, stop=True)
            last.then_inc(xT_done, 1)
            pe.wait_ge(xT_saved, 1)
            nc.tensor.matmul(max_ps[:, 0, 0:TOK], wq_sb[:, :], xnT[:, :], start=True, stop=True).then_inc(q_done, 1)
            pe.wait_ge(ctx_loaded[1], 16)
            for n in range(NCH):
                pe.wait_ge(k_low_saved, n + 1)
                k_project(1, 1, n, score_ps[:, n // 2, n % 2, :])
            pe.wait_ge(cleared, 1)
            for n in range(3):
                if n:
                    pe.wait_ge(v_saved, n)
                v_project(0, n)
            pe.wait_ge(q_low_saved, 1)
            pe.wait_ge(qx_ready, 1)
            for n in range(MN):
                if part_of(n) is not None:
                    pe.wait_ge(kx_loaded[0][part_of(n)], MOVES)
                max_scores(0, 0, n)
            pe.wait_ge(v_saved, 3)
            transpose_max(3)
            pe.wait_ge(nm_rows, 1)
            pe.wait_ge(k_low_saved, 2 * NCH)
            scores(0, 0, 0)
            scores(0, 0, 2)

            def body(i, par, keys_next=True, next_batch=True):
                b = batch(i, par)
                i1, par1 = nxt(i, par, 1)
                for t in range(KT):
                    chunks = list(MAX_STEPS[t]) if next_batch else []

                    def one_chunk():
                        if chunks:
                            n = chunks.pop(0)
                            moved, _ = counts(pe, MOVES * (i1 + 1), MN * (b + 1) + n - 1)
                            staged, spread = counts(pe, b + 2, b + 1)
                            if n == 0:
                                pe.wait_ge(qx_ready, staged)
                            if n == 1:
                                pe.wait_ge(den_taken, spread)
                            if part_of(n) is not None:
                                pe.wait_ge(kx_loaded[par1][part_of(n)], moved)
                            max_scores(b + 1, par1, n)

                    if next_batch and t == NM_STEP:
                        taken, ready = counts(pe, 3 * (b + 2), 3 * (b + 2))
                        pe.wait_ge(v_saved, taken)
                        transpose_max(ready)
                    if t == KT - 1 and next_batch:
                        pe.wait_ge(nm_rows, b + 2)
                    for g0 in (0, 2):
                        if t < KT - 1:
                            scores(par, t + 1, g0)
                        elif next_batch:
                            scores(par1, 0, g0)
                        one_chunk()
                    if next_batch and t in V_STEPS:
                        n = V_STEPS.index(t)
                        if n == 0:
                            rows, split = counts(pe, b + 1, NCH * (b + 2))
                            pe.wait_ge(nm_rows, rows)
                            pe.wait_ge(k_low_saved, split)
                        elif keys_next:
                            pe.wait_ge(k_low_saved, NCH * (b + 2) + n)
                        else:
                            pe.wait_ge(v_saved, 3 * (b + 1) + n)
                        v_project(par1, n)
                    if keys_next and t in K_STEPS and t < KT - 1:
                        n = K_STEPS.index(t)
                        loaded, taken = counts(pe, 16 * (i + 2), 3 * (b + 1) + n + 1)
                        if n == 0:
                            pe.wait_ge(ctx_loaded[par], loaded)
                        pe.wait_ge(v_saved, taken)
                        k_project(b + 2, par, n, misc_ps)
                    pe.wait_ge(exp_done, KT * b + t + 1)
                    attend(par, t, 0)
                    one_chunk()
                    last = attend(par, t, 1)
                    if t == KT - 1:
                        last.then_inc(pv_done, 1)
                    while chunks:
                        one_chunk()
                if keys_next:
                    pe.wait_ge(nm_rows, b + 2)
                    k_project(b + 2, par, NCH - 1, misc_ps)
                saved, taken = counts(pe, b + 1, MN * (b + 2))
                pe.wait_ge(o_saved, saved)
                if next_batch:
                    pe.wait_ge(max_taken, taken)
                nc.tensor.matmul(max_ps[:, 1, 0:2 * PC], den_sel[:, :], o_sb[:, :], start=True, stop=True
                                 ).then_inc(den_done, 1)

            with pe.Fori(0, B // 2 - 1) as i:
                body(i, 0)
                body(i, 1)
            body(3, 0, keys_next=False)
            body(3, 1, keys_next=False, next_batch=False)

            pe.wait_ge(wo_loaded, 16 * H)
            pe.wait_ge(exp_done, KT * B)
            pe.wait_ge(o_norm_ready, B + 1)
            for r in range(NR):
                for s in range(2):
                    for i in range(2):
                        last = nc.tensor.matmul(score_ps[0:RT, r // 2, r % 2, 0:D], o_norm[:, r, 2 * s + i, :, :].rearrange("p b c -> p (b c)"),
                                                wo_sb[:, 2 * s + i, :], start=(s + i == 0), stop=(s + i == 2))
                last.then_inc(wo_done, 1)
            for r in range(NR):
                pe.wait_ge(xn_ready, NR + r + 1)
                last = nc.tensor.matmul(misc_ps[:, RT * r:RT * r + RT], xn[:, r, :], ident[0:RT, 0:RT],
                                        start=True, stop=True)
            last.then_inc(xT_done, 1)
            pe.wait_ge(xT_saved, 2)
            pe.wait_ge(ffn_loaded, 48)
            for r in range(NR):
                nc.tensor.matmul(max_ps[0:RT, 0, E * r:E * r + E], xnT[:, RT * r:RT * r + RT], gw_sb[:, :],
                                 start=True, stop=True).then_inc(logits_done, 1)

            def gate(n):
                e, j = n // FT, n % FT
                if n >= 2:
                    pe.wait_ge(gelu_ready, n - 1)
                nc.tensor.matmul(score_ps[:, n % 2, 0, 0:TOK], gu_sb[:, e, 128 * j:128 * j + 128], xnT[:, :],
                                 start=True, stop=True).then_inc(gate_done, 1)

            def up(n):
                e, j = n // FT, n % FT
                pe.wait_ge(xe_ready, e + 1)
                if n >= 2:
                    pe.wait_ge(hact_ready, n - 1)
                nc.tensor.matmul(score_ps[:, n % 2, 1, 0:TOK], gu_sb[:, e, F + 128 * j:F + 128 * j + 128],
                                 x_expert[:, e % 2, :], start=True, stop=True).then_inc(up_done, 1)

            def spread_weight(e):
                if e >= 2:
                    pe.wait_ge(xe_ready, e - 1)
                nc.tensor.matmul(max_ps[:, e % 2, 0:TOK], expert_sel[:, e, :], combT, start=True, stop=True
                                 ).then_inc(bc_done, 1)

            def down(n):
                pe.wait_ge(hact_ready, n + 1)
                nc.tensor.matmul(o_ps[:, 0:TOK], dn_sb[:, n // FT, n % FT, :], hact[:, n % 2, :],
                                 start=(n == 0), stop=(n == E * FT - 1)).then_inc(down_done, 1)

            gate(0)
            gate(1)
            pe.wait_ge(comb_ready, 1)
            for r in range(NR):
                last = nc.tensor.matmul(max_ps[0:16, 1, RT * r:RT * r + RT],
                                        comb_parts[:, r, :, :].bitcast(f32).rearrange("t a e -> t (a e)"),
                                        ident[0:RT, 0:RT], start=True, stop=True)
            last.then_inc(combT_done, 1)
            pe.wait_ge(combT_saved, 1)
            spread_weight(0)
            spread_weight(1)
            for n in range(E * FT):
                up(n)
                if n + 2 < E * FT:
                    gate(n + 2)
                if n >= 1:
                    down(n - 1)
                if n % FT == FT - 1 and n // FT + 2 < E:
                    spread_weight(n // FT + 2)
            down(E * FT - 1)
            pe.wait_ge(y_saved, 1)
            for r in range(NR):
                nc.tensor.matmul(score_ps[0:RT, r // 2, r % 2, 0:D], yT[:, RT * r:RT * r + RT], ident[:, :],
                                 start=True, stop=True).then_inc(yT_done, 1)


V_STEPS = [0, 4, 8]
K_STEPS = [2, 6, 11]
NM_STEP = 10
MAX_STEPS = [[0], [1, 2, 3], [4, 5, 6], [7, 8, 9], [10, 11, 12], [13, 14, 15], [16, 17, 18], [19, 20, 21], [22, 23], [], [], []]


def kernel(x, ctx_1024, g_xattn, g_ffn, L0_xattn_w_q, L0_xattn_w_k, L0_xattn_w_v, L0_xattn_w_o,
           L0_ffn_gate_w, L0_ffn_gate_up_w, L0_ffn_down_w):
    import numpy as np
    import concourse.bacc as bacc
    from concourse.bass_utils import run_bass_kernel_spmd

    layout = np.ascontiguousarray
    arrays = {
        "x": layout(np.asarray(x).reshape(NR, RT, D).transpose(1, 0, 2)),
        "ctxT": layout(np.asarray(ctx_1024).transpose(0, 2, 1)),
        "g_attn": np.asarray(g_xattn),
        "g_ffn": np.asarray(g_ffn),
        "wqT": layout(np.asarray(L0_xattn_w_q).T),
        "wkT": layout(np.asarray(L0_xattn_w_k).T),
        "wvT": layout(np.asarray(L0_xattn_w_v).T),
        "woT": layout(np.asarray(L0_xattn_w_o).T),
        "gwT": layout(np.asarray(L0_ffn_gate_w).T),
        "guT": layout(np.asarray(L0_ffn_gate_up_w).transpose(2, 0, 1)),
        "dnT": layout(np.asarray(L0_ffn_down_w).reshape(E, D, FT, 128).transpose(3, 0, 2, 1)),
    }
    nc = bacc.Bacc("TRN2", target_bir_lowering=False, num_devices=1)
    f32 = mybir.dt.float32
    args = [nc.dram_tensor(f"in_{n}", a.shape, f32, kind="ExternalInput").ap() for n, a in arrays.items()]
    result = nc.dram_tensor("out_0", (RT, NR, D), f32, kind="ExternalOutput").ap()
    flamingo_block(nc, *args, result)
    ran = run_bass_kernel_spmd(nc, [{f"in_{n}": a for n, a in arrays.items()}], core_ids=[0])
    return ran.results[0]["out_0"].transpose(1, 0, 2).reshape(B, TQ, D)
```

```python
from contextlib import ExitStack

import concourse.bass as bass
from concourse import mybir

B, TQ, D = 8, 56, 128
TK = 1500
H, HD = 16, 8
E, F = 8, 512
EPS = 1e-5
SCALE = HD ** -0.5

TOK = B * TQ
NR = 4
RT = TOK // NR
KT = -(-TK // 128)
LAST = TK - 128 * (KT - 1)
KPAD = 128 * KT
NCH = 3
CK = 512
HT = 8
HALF = [(0, 128 * HT), (128 * HT, TK - 128 * HT)]
G, GC = 4, 4 * TQ
NP, PC = 8, 2 * TQ
SC = H * TQ
VP = 17
VW = VP * (NP - 1) + 32
MR = 96
KR = 112
MOVES = 16 * 6
NB = 3
NHS = 2 * KT
MN = NCH * NP
FT = F // 128


def chunk(n):
    return CK * n, min(CK, TK - CK * n)


def max_product(n):
    return (n // 2, n % 2) if n < 2 * NP else (n - 2 * NP, 2)


def keys_of(n):
    return {0: (0, 0), NP: (0, 1), 2 * NP: (1, 0), 2 * NP + NP // 2: (1, 1)}.get(n)


def flamingo_block(nc, x, ctxT, g_attn, g_ffn, wqT, wkT, wvT, woT, gwT, guT, dnT, out):
    f32, f32r = mybir.dt.float32, mybir.dt.float32r
    ALU, ACT, AX = mybir.AluOpType, mybir.ActivationFunctionType, mybir.AxisListType

    with ExitStack() as stack:
        def sb(name, shape, dt=f32):
            return stack.enter_context(nc.sbuf_tensor(name, shape, dt))

        def pb(name, shape):
            return stack.enter_context(nc.psum_tensor(name, shape, f32))

        def sem(name):
            return stack.enter_context(nc.semaphore(name))

        kx = sb("kx", [128, 2, G, KPAD], f32r)
        qx = sb("qx", [128, 2, G, GC], f32r)
        q_parts = sb("q_parts", [MR, G, TOK], f32r)
        k_high = sb("k_high", [128, KPAD], f32r)
        k_low = sb("k_low", [128, KPAD], f32r)
        k_full = sb("k_full", [128, KPAD])
        ctx_sb = sb("ctx_sb", [128, 2, KPAD])
        v_sb = sb("v_sb", [128, 2, KT, VW])
        probs = sb("probs", [128, 2, SC])
        o_sb = sb("o_sb", [128, 2 * PC])
        o_norm = sb("o_norm", [128, NR, 4, 2, TQ])
        inv_den = sb("inv_den", [128, 2 * PC])
        part_max = sb("part_max", [PC, NP, NCH])
        neg_max = sb("neg_max", [PC, NP])
        neg_max_parts = sb("neg_max_parts", [PC, 2, NP], f32r)
        wq_sb, wk_sb, wv_sb = sb("wq_sb", [D, G, MR]), sb("wk_sb", [D, D]), sb("wv_sb", [D, D])
        wo_sb = sb("wo_sb", [128, 4, D])
        gw_sb = sb("gw_sb", [D, E])
        gu_sb = sb("gu_sb", [D, E, 2 * F])
        dn_sb = sb("dn_sb", [128, E, FT, D])
        x_sb = sb("x_sb", [RT, NR, D])
        xn = sb("xn", [RT, NR, D])
        xnT = sb("xnT", [D, TOK])
        x1 = sb("x1", [RT, NR, D])
        stats = sb("stats", [RT, NR, 6])
        mean_var = sb("mean_var", [RT, NR, 2])
        var_eps = sb("var_eps", [RT, NR])
        rstd = sb("rstd", [RT, NR])
        minus_half = sb("minus_half", [RT, NR])
        gates = sb("gates", [128, 2])
        tanh_g = sb("tanh_g", [128, 2])
        ident = sb("ident", [128, 128])
        head_mask3 = sb("head_mask3", [128, G, 4])
        head_mask = sb("head_mask", [128, 4])
        den_sel = sb("den_sel", [128, 128])
        row_mask = sb("row_mask", [16, NP])
        expert_sel = sb("expert_sel", [16, E, 128], f32r)
        before = sb("before", [RT, E, E])
        logits = sb("logits", [RT, NR, E])
        row8 = sb("row8", [RT, 4, NR])
        pr = sb("pr", [RT, NR, E])
        rank = sb("rank", [RT, NR, E])
        comb = sb("comb", [RT, NR, E])
        comb_parts = sb("comb_parts", [RT, NR, 2, E], f32r)
        combT = q_parts[0:16, 0, :]
        out_sb = xn
        o_flat = o_norm[:, :, :, :, :].rearrange("p r s b c -> p (r s b c)")
        greater = ctx_sb[0:RT, 0, 0:NR * E * E].rearrange("t (r e j) -> t r e j", r=NR, e=E)
        equal = ctx_sb[0:RT, 1, 0:NR * E * E].rearrange("t (r e j) -> t r e j", r=NR, e=E)
        gelu_sb = probs[:, 0, :].rearrange("p (a t) -> p a t", a=2)
        hact = probs[:, 1, :].rearrange("p (a t) -> p a t", a=2)
        x_expert = o_flat[:, 0:2 * TOK].rearrange("p (a t) -> p a t", a=2)
        yT = o_flat[:, 2 * TOK:3 * TOK]

        score_ps = pb("score_ps", [128, NB, 512])
        max_ps = pb("max_ps", [128, NB, 512])
        o_ps = pb("o_ps", [128, 512])
        misc_ps = pb("misc_ps", [128, 512])
        q_banks = [max_ps[:, 0, :], max_ps[:, 1, :], max_ps[:, 2, :], o_ps[:, :]]
        token_banks = [score_ps[:, 0, :], score_ps[:, 1, :], score_ps[:, 2, :], o_ps[:, :]]
        gate_banks = [score_ps[:, 0, :], score_ps[:, 1, :]]
        up_banks = [score_ps[:, 2, :], misc_ps[:, :]]
        out_banks = gate_banks + up_banks

        x_loaded, w_loaded, wo_loaded, ffn_loaded, g_loaded = map(sem, ("x_loaded", "w_loaded", "wo_loaded", "ffn_loaded", "g_loaded"))
        ctx_loaded = [sem("ctx_loaded0"), sem("ctx_loaded1")]
        kx_loaded = [[[sem(f"kx_loaded{p}{h}{g}") for g in range(2)] for h in range(2)] for p in range(2)]
        consts, mask_ready, cleared, wo_cleared, pool_step = map(sem, ("consts", "mask_ready", "cleared", "wo_cleared", "pool_step"))
        var_ready, rstd_ready, xn_ready, xT_done, xT_saved = map(sem, ("var_ready", "rstd_ready", "xn_ready", "xT_done", "xT_saved"))
        q_done, q_high_saved, q_low_saved = map(sem, ("q_done", "q_high_saved", "q_low_saved"))
        k_done, k_saved, k_low_saved = map(sem, ("k_done", "k_saved", "k_low_saved"))
        v_done, v_saved = map(sem, ("v_done", "v_saved"))
        kx_ones, qx_ready = sem("kx_ones"), sem("qx_ready")
        scores_done, exp_done, pv_done = map(sem, ("scores_done", "exp_done", "pv_done"))
        max_done, max_taken = map(sem, ("max_done", "max_taken"))
        nm_step, nmT_done, nm_rows = map(sem, ("nm_step", "nmT_done", "nm_rows"))
        o_saved, den_done, den_taken, o_norm_ready = map(sem, ("o_saved", "den_done", "den_taken", "o_norm_ready"))
        ln_step, tanh_ready = map(sem, ("ln_step", "tanh_ready"))
        wo_done, x1_ready = map(sem, ("wo_done", "x1_ready"))
        logits_done, logits_exp, router_step, comb_ready = map(sem, ("logits_done", "logits_exp", "router_step", "comb_ready"))
        combT_done, combT_saved = map(sem, ("combT_done", "combT_saved"))
        bc_done, xe_ready = map(sem, ("bc_done", "xe_ready"))
        gate_done, up_done, gelu_ready, hact_ready, down_done = map(sem, ("gate_done", "up_done", "gelu_ready", "hact_ready", "down_done"))
        y_saved, yT_done, out_ready, stored = map(sem, ("y_saved", "yT_done", "out_ready", "stored"))

        block = stack.enter_context(nc.Block())

        def bc(ap, shape):
            return ap.to_broadcast(shape)

        def nxt(i, par, k):
            return i + (par + k) // 2, (par + k) % 2

        def batch(i, par):
            return 2 * i + par

        def counts(eng, *values):
            for v in values:
                if not isinstance(v, int):
                    eng.lower_val(v)
            return values

        def block_diagonal(eng, b, par):
            src = q_parts[:, :, bass.ds(TQ * b, TQ)].bitcast(f32).unsqueeze(2)
            mask = head_mask[0:MR, :].unsqueeze(1).unsqueeze(3)
            return eng.tensor_tensor(qx[0:MR, par, :, :].rearrange("p g (h c) -> p g h c", h=4),
                                     bc(src, [MR, G, 4, TQ]), bc(mask, [MR, G, 4, TQ]), ALU.mult)

        @block.sync
        def _(sp):
            def move_keys(par, part):
                start, size = HALF[part]
                for g in range(G):
                    for row, src in ((0, k_high), (1, k_low), (2, k_high)):
                        sp.dma_start(kx[32 * row:32 * row + 32, par, g, start:start + size].bitcast(f32),
                                     src[32 * g:32 * g + 32, start:start + size].bitcast(f32)
                                     ).then_inc(kx_loaded[par][part][g // 2], 16)

            sp.dma_start(x_sb[:, :, :], x).then_inc(x_loaded, 16)
            sp.dma_start(wk_sb[:, :], wkT).then_inc(w_loaded, 16)
            sp.dma_start(ctx_sb[:, 0, 0:TK], ctxT[0]).then_inc(ctx_loaded[0], 16)
            sp.dma_start(ctx_sb[:, 1, 0:TK], ctxT[1]).then_inc(ctx_loaded[1], 16)
            for half in range(2):
                sp.wait_ge(k_low_saved, 2 + half)
                move_keys(0, half)
            sp.wait_ge(k_low_saved, NCH + 2)
            move_keys(1, 0)
            sp.wait_ge(v_done, 3)
            sp.dma_start(ctx_sb[:, 0, 0:TK], ctxT[2]).then_inc(ctx_loaded[0], 16)
            sp.wait_ge(wo_cleared, 1)
            for s in range(2):
                for i in range(2):
                    for j in range(4):
                        h = 2 * (4 * s + j) + i
                        r = 32 * j + HD * i
                        sp.dma_start(wo_sb[r:r + HD, 2 * s + i, :], woT[HD * h:HD * h + HD, :]).then_inc(wo_loaded, 16)

            def body(i, par, ctx_next=True, keys_next=True):
                b = batch(i, par)
                par1 = 1 - par
                split_2, split_1, left_2, left_1, taken = counts(
                    sp, NCH * (b + 2), NCH * (b + 2) + 2, NHS * b + 1, NHS * b + 2 * HT, 3 * (b + 2))
                sp.wait_ge(k_low_saved, split_2)
                sp.wait_ge(scores_done, left_2)
                move_keys(par1, 1)
                if keys_next:
                    sp.wait_ge(k_low_saved, split_1)
                    sp.wait_ge(scores_done, left_1)
                    move_keys(par, 0)
                if ctx_next:
                    sp.wait_ge(v_done, taken)
                    sp.dma_start(ctx_sb[:, par1, 0:TK], ctxT[b + 3]).then_inc(ctx_loaded[par1], 16)
                load_expert(b)

            def load_expert(e):
                sp.dma_start(gu_sb[:, e, :], guT[:, e, :]).then_inc(ffn_loaded, 16)
                sp.dma_start(dn_sb[:, e, :, :], dnT[:, e, :, :]).then_inc(ffn_loaded, 16)

            with sp.Fori(0, 2) as i:
                body(i, 0)
                body(i, 1)
            body(2, 0)
            body(2, 1, ctx_next=False)
            body(3, 0, ctx_next=False, keys_next=False)
            for e in range(B - 1, E):
                load_expert(e)
            sp.wait_ge(out_ready, NR)
            sp.dma_start(out, out_sb[:, :, :]).then_inc(stored, 16)
            sp.wait_ge(stored, 16)

        @block.gpsimd
        def _(pool):
            steps = [0]

            def serial(ins):
                steps[0] += 1
                ins.then_inc(pool_step, 1)
                pool.wait_ge(pool_step, steps[0])

            serial(nc.gpsimd.memset(minus_half[:, :], -0.5))
            serial(nc.gpsimd.memset(ident[:, :], 0.0))
            serial(nc.gpsimd.affine_select(out=ident[:, :], in_=ident[:, :], compare_op=ALU.not_equal, fill=1.0,
                                           base=0, pattern=[[-1, 128]], channel_multiplier=1))
            serial(nc.gpsimd.memset(head_mask3[:, :, :], 1.0))
            serial(nc.gpsimd.affine_select(out=head_mask3[:, :, :], in_=head_mask3[:, :, :], compare_op=ALU.is_ge,
                                           fill=0.0, base=0, pattern=[[-32, G], [-HD, 4]], channel_multiplier=1))
            serial(nc.gpsimd.affine_select(out=head_mask3[:, :, :], in_=head_mask3[:, :, :], compare_op=ALU.is_ge,
                                           fill=0.0, base=HD - 1, pattern=[[32, G], [HD, 4]], channel_multiplier=-1))
            serial(nc.gpsimd.memset(row_mask[:, :], 0.0))
            for r in (0, NP):
                serial(nc.gpsimd.affine_select(out=row_mask[:, :], in_=row_mask[:, :], compare_op=ALU.not_equal,
                                               fill=1.0, base=-r, pattern=[[-1, NP]], channel_multiplier=1))
            serial(nc.gpsimd.memset(den_sel[:, :], 0.0))
            sel = den_sel[:, :].rearrange("k (j m) -> k j m", j=4)
            serial(nc.gpsimd.affine_select(out=sel, in_=sel, compare_op=ALU.not_equal, fill=1.0,
                                           base=-16, pattern=[[-32, 4], [0, 32]], channel_multiplier=1))
            serial(nc.gpsimd.memset(before[:, :, :], 1.0))
            nc.gpsimd.affine_select(out=before[:, :, :], in_=before[:, :, :], compare_op=ALU.is_ge, fill=0.0,
                                    base=-1, pattern=[[1, E], [-1, E]], channel_multiplier=0).then_inc(consts, 1)
            pool.wait_ge(consts, 1)
            pool.wait_ge(var_ready, 1)
            nc.gpsimd.tensor_tensor(rstd[:, :], var_eps[:, :], minus_half[:, :], ALU.pow).then_inc(rstd_ready, 1)

            def stage(b, par):
                block_diagonal(nc.gpsimd, b, par).then_inc(qx_ready, 1)

            def k_rest(b, n, part=None, move_count=0):
                start, size = chunk(n)
                saved, move_count = counts(pool, 2 * (NCH * b + n + 1), move_count)
                pool.wait_ge(k_saved, saved)
                nc.gpsimd.tensor_tensor(k_low[:, start:start + size], k_full[:, start:start + size],
                                        k_high[:, start:start + size].bitcast(f32), ALU.subtract
                                        ).then_inc(k_low_saved, 1)

            pool.wait_ge(rstd_ready, 1)
            nc.gpsimd.memset(kx[MR:128, :, :, :].bitcast(f32), 1.0).then_inc(kx_ones, 1)
            pool.wait_ge(kx_ones, 1)
            pool.wait_ge(mask_ready, 1)
            pool.wait_ge(q_low_saved, G)
            pool.wait_ge(qx_ready, 1)
            stage(1, 1)

            def body(i, par):
                b = batch(i, par)
                for n in range(NCH):
                    if n == NCH - 1:
                        staged, left = counts(pool, b + 2, NHS * (b + 1))
                        pool.wait_ge(qx_ready, staged)
                        pool.wait_ge(scores_done, left)
                        stage(b + 2, par)
                    k_rest(b + 2, n)

            with pool.Fori(0, B // 2 - 1) as i:
                body(i, 0)
                body(i, 1)
            pool.wait_ge(qx_ready, B)
            pool.wait_ge(var_ready, 2)
            nc.gpsimd.tensor_tensor(rstd[:, :], var_eps[:, :], minus_half[:, :], ALU.pow).then_inc(rstd_ready, 1)

        @block.scalar
        def _(act):
            act.dma_start(wq_sb[:, :, :], wqT).then_inc(w_loaded, 16)
            act.dma_start(wv_sb[:, :], wvT).then_inc(w_loaded, 16)
            act.dma_start(gates[:, 0:1], g_attn.partition_broadcast(128)).then_inc(g_loaded, 16)
            act.dma_start(gates[:, 1:2], g_ffn.partition_broadcast(128)).then_inc(g_loaded, 16)
            act.dma_start(gw_sb[:, :], gwT).then_inc(ffn_loaded, 16)
            act.wait_ge(g_loaded, 32)
            nc.scalar.activation(tanh_g[:, :], gates[:, :], ACT.Tanh).then_inc(tanh_ready, 1)

            def k_copy(b, n, bank, par=None, move_count=0, whole=True):
                start, size = chunk(n)
                projected, move_count = counts(act, NCH * b + n + 1, move_count)
                if par is not None and n != 1:
                    act.wait_ge(kx_loaded[par][n // 2][0], move_count)
                    act.wait_ge(kx_loaded[par][n // 2][1], move_count)
                act.wait_ge(k_done, projected)
                nc.scalar.activation(k_high[:, start:start + size], bank[:, 0:size], ACT.Copy
                                     ).then_inc(k_saved, 1 if whole else 2)
                if whole:
                    nc.scalar.activation(k_full[:, start:start + size], bank[:, 0:size], ACT.Copy).then_inc(k_saved, 1)

            def v_copy(b, par, n):
                act.wait_ge(v_done, 3 * b + n + 1)
                dst = v_sb[:, par, 4 * n:4 * n + 4, 0:VP * NP].rearrange("k t (p c) -> k t p c", p=NP)[:, :, :, 0:16]
                src = misc_ps[:, :].rearrange("k (t p c) -> k t p c", t=4, p=NP)
                nc.scalar.activation(dst, src, ACT.Copy).then_inc(v_saved, 1)

            def exp_half(b, hs):
                t, h = hs // 2, hs % 2
                act.wait_ge(scores_done, NHS * b + hs + 1)
                m = 128 if t < KT - 1 else LAST
                nc.scalar.activation(probs[0:m, t % 2, SC // 2 * h:SC // 2 * (h + 1)], score_ps[0:m, hs % NB, 0:SC // 2],
                                     ACT.Exp, scale=SCALE).then_inc(exp_done, 1)

            for n in range(NCH):
                k_copy(0, n, score_ps[:, n, :], whole=False)
            act.wait_ge(xT_done, 1)
            nc.scalar.activation(xnT[:, :], misc_ps[:, 0:TOK], ACT.Copy).then_inc(xT_saved, 1)
            for g in range(G):
                act.wait_ge(q_done, g + 1)
                nc.scalar.activation(q_parts[:, g, :], q_banks[g][0:MR, 0:TOK], ACT.Copy).then_inc(q_high_saved, 1)
            act.wait_ge(cleared, 2)
            for n in range(NCH):
                v_copy(0, 0, n)
                k_copy(1, n, score_ps[:, n, :], 0, MOVES, whole=False)
            exp_half(0, 0)
            exp_half(0, 1)

            def body(i, par, keys_next=True, next_batch=True):
                b = batch(i, par)
                i1, par1 = nxt(i, par, 1)
                for t in range(KT):
                    for h in range(2):
                        if t < KT - 1:
                            exp_half(b, 2 * t + 2 + h)
                        elif next_batch:
                            exp_half(b + 1, h)
                    job, n = JOBS.get(t, (None, None))
                    if next_batch and job == "V":
                        v_copy(b + 1, par1, n)
                    if keys_next and job == "K":
                        k_copy(b + 2, n, misc_ps, par1, MOVES * (i1 + 1))

            with act.Fori(0, B // 2 - 1) as i:
                body(i, 0)
                body(i, 1)
            body(3, 0, keys_next=False)
            body(3, 1, keys_next=False, next_batch=False)

            act.wait_ge(xT_done, 2)
            nc.scalar.activation(xnT[:, :], misc_ps[:, 0:TOK], ACT.Copy).then_inc(xT_saved, 1)
            act.wait_ge(router_step, 2)
            nc.scalar.activation(pr[:, :, :], logits[:, :, :], ACT.Exp).then_inc(logits_exp, 1)
            act.wait_ge(combT_done, 1)
            nc.scalar.activation(combT, max_ps[0:16, 2, 0:TOK], ACT.Copy).then_inc(combT_saved, 1)
            for n in range(E * FT):
                act.wait_ge(gate_done, n + 1)
                if n >= 2:
                    act.wait_ge(hact_ready, n - 1)
                nc.scalar.activation(gelu_sb[:, n % 2, :], gate_banks[n % 2][:, 0:TOK], ACT.Gelu).then_inc(gelu_ready, 1)
            act.wait_ge(down_done, E * FT)
            nc.scalar.activation(yT, o_ps[:, 0:TOK], ACT.Copy).then_inc(y_saved, 1)

        @block.vector
        def _(dve):
            ln = [0]

            def layer_norm(src, turn):
                for r in range(NR):
                    nc.vector.bn_stats(stats[:, r, :], src[:, r, :]).then_inc(ln_step, 1)
                    ln[0] += 1
                dve.wait_ge(ln_step, ln[0])
                for r in range(NR):
                    nc.vector.bn_aggr(mean_var[:, r, :], stats[:, r, :]).then_inc(ln_step, 1)
                    ln[0] += 1
                dve.wait_ge(ln_step, ln[0])
                nc.vector.tensor_scalar(var_eps[:, :], mean_var[:, :, 1], EPS, None, ALU.add).then_inc(var_ready, 1)
                dve.wait_ge(rstd_ready, turn)
                for r in range(NR):
                    nc.vector.tensor_scalar(xn[:, r, :], src[:, r, :], mean_var[:, r, 0:1], rstd[:, r:r + 1],
                                            ALU.subtract, ALU.mult).then_inc(xn_ready, 1)

            def k_rest(b, n, bank):
                start, size = chunk(n)
                dve.wait_ge(k_saved, 2 * (NCH * b + n + 1))
                nc.vector.tensor_tensor(k_low[:, start:start + size], bank[:, 0:size],
                                        k_high[:, start:start + size].bitcast(f32), ALU.subtract
                                        ).then_inc(k_low_saved, 1)

            def take_max(b, n):
                p, c = max_product(n)
                size = chunk(c)[1]
                dve.wait_ge(max_done, MN * b + n + 1)
                nc.vector.reduce_max(part_max[:, p, c:c + 1], max_ps[0:PC, n % NB, 0:size],
                                     AX.X).then_inc(max_taken, 1)

            def negate_max(b):
                dve.wait_ge(max_taken, MN * (b + 1))
                nc.vector.tensor_reduce(neg_max[:, :], part_max[:, :, :], AX.X, ALU.max, negate=True).then_inc(nm_step, 1)
                dve.wait_ge(nm_step, 3 * b + 1)
                nc.vector.tensor_copy(neg_max_parts[:, 0, :], neg_max[:, :]).then_inc(nm_step, 1)
                dve.wait_ge(nm_step, 3 * b + 2)
                nc.vector.tensor_tensor(neg_max_parts[:, 1, :], neg_max[:, :], neg_max_parts[:, 0, :].bitcast(f32),
                                        ALU.subtract).then_inc(nm_step, 1)

            def max_rows(b, par):
                dve.wait_ge(nmT_done, b + 1)
                for h in range(2):
                    dst = qx[MR:KR, par, 2 * h:2 * h + 2, :].rearrange("r g (p c) -> r (g p) c", p=2)
                    half = [16, NP // 2, PC]
                    nc.vector.tensor_tensor(dst, bc(max_ps[0:16, 0, 0:PC].unsqueeze(1), half),
                                            bc(row_mask[:, NP // 2 * h:NP // 2 * (h + 1)].unsqueeze(2), half), ALU.mult
                                            ).then_inc(nm_rows, 1)

            nc.vector.memset(ctx_sb[:, 0, TK:KPAD], 0.0).then_inc(o_norm_ready, 1)
            nc.vector.memset(ctx_sb[:, 1, TK:KPAD], 0.0).then_inc(den_taken, 1)
            values = v_sb[:, :, :, 0:VP * NP].rearrange("k a t (p c) -> k (a t) p c", p=NP)
            nc.vector.memset(values[:, :, :, VP - 1:VP], 1.0).then_inc(cleared, 1)
            nc.vector.memset(v_sb[:, :, :, VP * NP:VW], 1.0).then_inc(cleared, 1)
            nc.vector.memset(wo_sb[:, :, :], 0.0).then_inc(wo_cleared, 1)
            dve.wait_ge(x_loaded, 16)
            layer_norm(x_sb, 1)
            dve.wait_ge(consts, 1)
            nc.vector.tensor_copy(expert_sel[:, :, :], bc(row_mask[:, :].unsqueeze(2), [16, E, 128]))
            for n in range(NCH):
                k_rest(0, n, score_ps[:, n, :])
            nc.vector.tensor_reduce(head_mask[:, :], head_mask3[:, :, :].rearrange("p g h -> p h g"), AX.X,
                                    ALU.add).then_inc(mask_ready, 1)
            for g in range(G):
                dve.wait_ge(q_high_saved, g + 1)
                low = q_parts[64:MR, g, :]
                nc.vector.tensor_tensor(low, q_banks[g][64:MR, 0:TOK], low.bitcast(f32),
                                        ALU.subtract).then_inc(q_low_saved, 1)
            dve.wait_ge(mask_ready, 1)
            dve.wait_ge(q_low_saved, G)
            block_diagonal(nc.vector, 0, 0).then_inc(qx_ready, 1)
            for n in range(MN):
                take_max(0, n)
                if n in FIRST_SPLITS:
                    k_rest(1, FIRST_SPLITS.index(n), score_ps[:, FIRST_SPLITS.index(n), :])
            negate_max(0)
            max_rows(0, 0)

            def body(i, par, next_batch=True):
                b = batch(i, par)
                par1 = 1 - par
                for t in range(KT):
                    for n in (MAX_STEPS[t] if next_batch else ()):
                        take_max(b + 1, n)
                    if next_batch and t == NM_STEP:
                        negate_max(b + 1)
                        max_rows(b + 1, par1)
                complete, normalised = counts(dve, b + 1, b + 1)
                dve.wait_ge(o_norm_ready, normalised)
                dve.wait_ge(pv_done, complete)
                nc.vector.tensor_copy(o_sb[:, :], o_ps[:, 0:2 * PC]).then_inc(o_saved, 1)
                dve.wait_ge(den_done, b + 1)
                nc.vector.reciprocal(inv_den[:, :], max_ps[:, 2, 0:2 * PC]).then_inc(den_taken, 1)
                dve.wait_ge(den_taken, b + 2)
                four = "p (s c) -> p s c"
                nc.vector.tensor_tensor(o_norm[:, i, :, par, :], o_sb[:, :].rearrange(four, s=4),
                                        inv_den[:, :].rearrange(four, s=4), ALU.mult).then_inc(o_norm_ready, 1)

            with dve.Fori(0, B // 2 - 1) as i:
                body(i, 0)
                body(i, 1)
            body(3, 0)
            body(3, 1, next_batch=False)

            dve.wait_ge(tanh_ready, 1)
            for r in range(NR):
                dve.wait_ge(wo_done, r + 1)
                nc.vector.scalar_tensor_tensor(x1[:, r, :], token_banks[r][0:RT, 0:D], tanh_g[0:RT, 0:1],
                                               x_sb[:, r, :], ALU.mult, ALU.add).then_inc(x1_ready, 1)
            dve.wait_ge(x1_ready, NR)
            layer_norm(x1, 2)

            steps = [0]

            def serial(ins):
                steps[0] += 1
                ins.then_inc(router_step, 1)
                dve.wait_ge(router_step, steps[0])

            dve.wait_ge(logits_done, NR)
            raw = max_ps[0:RT, 0, 0:NR * E].rearrange("t (r e) -> t r e", r=NR)
            big = [RT, NR, E]
            serial(nc.vector.reduce_max(row8[:, 0, :], raw, AX.X))
            serial(nc.vector.tensor_tensor(logits[:, :, :], raw, bc(row8[:, 0, :].unsqueeze(2), big), ALU.subtract))
            dve.wait_ge(logits_exp, 1)
            serial(nc.vector.tensor_reduce(row8[:, 1, :], pr[:, :, :], AX.X, ALU.add))
            serial(nc.vector.reciprocal(row8[:, 2, :], row8[:, 1, :]))
            serial(nc.vector.tensor_tensor(pr[:, :, :], pr[:, :, :], bc(row8[:, 2, :].unsqueeze(2), big), ALU.mult))
            cube = [RT, NR, E, E]
            other, own = bc(pr[:, :, :].unsqueeze(2), cube), bc(pr[:, :, :].unsqueeze(3), cube)
            serial(nc.vector.tensor_tensor(equal, other, own, ALU.is_equal))
            serial(nc.vector.tensor_tensor(greater, other, own, ALU.is_gt))
            serial(nc.vector.tensor_tensor(equal, equal, bc(before[:, :, :].unsqueeze(1), cube),
                                           ALU.mult))
            serial(nc.vector.tensor_tensor(greater, greater, equal, ALU.add))
            serial(nc.vector.tensor_reduce(rank[:, :, :], greater, AX.X, ALU.add))
            serial(nc.vector.scalar_tensor_tensor(comb[:, :, :], rank[:, :, :], 1.5, pr[:, :, :], ALU.is_lt, ALU.mult))
            serial(nc.vector.tensor_reduce(row8[:, 3, :], comb[:, :, :], AX.X, ALU.add))
            serial(nc.vector.reciprocal(row8[:, 1, :], row8[:, 3, :]))
            serial(nc.vector.tensor_tensor(comb[:, :, :], comb[:, :, :], bc(row8[:, 1, :].unsqueeze(2), big), ALU.mult))
            serial(nc.vector.tensor_copy(comb_parts[:, :, 0, :], comb[:, :, :]))
            nc.vector.tensor_tensor(comb_parts[:, :, 1, :], comb[:, :, :], comb_parts[:, :, 0, :].bitcast(f32),
                                    ALU.subtract).then_inc(comb_ready, 1)

            dve.wait_ge(xT_saved, 2)

            def scale_tokens(e):
                dve.wait_ge(bc_done, e + 1)
                nc.vector.tensor_tensor(x_expert[:, e % 2, :], max_ps[:, e % 2, 0:TOK], xnT[:, :], ALU.mult
                                        ).then_inc(xe_ready, 1)

            scale_tokens(0)
            for n in range(E * FT):
                if n % FT == 0 and n // FT + 1 < E:
                    scale_tokens(n // FT + 1)
                dve.wait_ge(gelu_ready, n + 1)
                dve.wait_ge(up_done, n + 1)
                if n >= 2:
                    dve.wait_ge(down_done, n - 1)
                nc.vector.tensor_tensor(hact[:, n % 2, :], up_banks[n % 2][:, 0:TOK], gelu_sb[:, n % 2, :],
                                        ALU.mult).then_inc(hact_ready, 1)
            for r in range(NR):
                dve.wait_ge(yT_done, r + 1)
                nc.vector.scalar_tensor_tensor(out_sb[:, r, :], out_banks[r][0:RT, 0:D], tanh_g[0:RT, 1:2],
                                               x1[:, r, :], ALU.mult, ALU.add).then_inc(out_ready, 1)

        @block.tensor
        def _(pe):
            def k_project(b, par, n, bank):
                start, size = chunk(n)
                nc.tensor.matmul(bank[:, 0:size], wk_sb[:, :], ctx_sb[:, par, start:start + size],
                                 start=True, stop=True).then_inc(k_done, 1)

            def v_project(par, n):
                for k in range(4):
                    t = 4 * n + k
                    last = nc.tensor.matmul(misc_ps[:, 128 * k:128 * k + 128], ctx_sb[:, par, 128 * t:128 * t + 128],
                                            wv_sb[:, :], start=True, stop=True)
                last.then_inc(v_done, 1)

            def scores(par, hs):
                t, h = hs // 2, hs % 2
                m = 128 if t < KT - 1 else LAST
                for g in (2 * h, 2 * h + 1):
                    last = nc.tensor.matmul(score_ps[0:m, hs % NB, GC * (g % 2):GC * (g % 2) + GC],
                                            kx[0:KR, par, g, 128 * t:128 * t + m], qx[0:KR, par, g, :],
                                            start=True, stop=True)
                last.then_inc(scores_done, 1)

            def max_scores(b, par, n):
                p, c = max_product(n)
                start, size = chunk(c)
                if n >= NB:
                    pe.wait_ge(max_taken, MN * b + n - NB + 1)
                nc.tensor.matmul(max_ps[0:PC, n % NB, 0:size], qx[0:MR, par, p // 2, PC * (p % 2):PC * (p % 2) + PC],
                                 kx[0:MR, par, p // 2, start:start + size], start=True, stop=True
                                 ).then_inc(max_done, 1)

            def attend(par, t, s):
                m = 128 if t < KT - 1 else LAST
                for j in range(4):
                    p = 4 * s + j
                    last = nc.tensor.matmul(o_ps[32 * j:32 * j + 32, PC * s:PC * s + PC],
                                            v_sb[0:m, par, t, VP * p:VP * p + 32],
                                            probs[0:m, t % 2, PC * p:PC * p + PC],
                                            start=(t == 0 and s == 0), stop=(t == KT - 1), skip_group_check=True)
                return last

            def transpose_max(ready):
                pe.wait_ge(nm_step, ready)
                nc.tensor.matmul(max_ps[0:16, 0, 0:PC], neg_max_parts[:, :, :].bitcast(f32).rearrange("t a p -> t (a p)"),
                                 ident[0:PC, 0:PC], start=True, stop=True).then_inc(nmT_done, 1)

            pe.wait_ge(w_loaded, 48)
            pe.wait_ge(ctx_loaded[0], 16)
            for n in range(NCH):
                k_project(0, 0, n, score_ps[:, n, :])
            pe.wait_ge(consts, 1)
            for r in range(NR):
                pe.wait_ge(xn_ready, r + 1)
                last = nc.tensor.matmul(misc_ps[:, RT * r:RT * r + RT], xn[:, r, :], ident[0:RT, 0:RT],
                                        start=True, stop=True)
            last.then_inc(xT_done, 1)
            pe.wait_ge(xT_saved, 1)
            for g in range(G):
                nc.tensor.matmul(q_banks[g][0:MR, 0:TOK], wq_sb[:, g, :], xnT[:, :], start=True, stop=True
                                 ).then_inc(q_done, 1)
            for n in range(-2, MN):
                if n == 0:
                    pe.wait_ge(q_low_saved, G)
                    pe.wait_ge(qx_ready, 1)
                if n >= 0 and keys_of(n) is not None:
                    part, groups = keys_of(n)
                    pe.wait_ge(kx_loaded[0][part][groups], MOVES)
                if n >= 0:
                    max_scores(0, 0, n)
                job, k = FIRST_JOBS.get(n, (None, 0))
                if job == "V":
                    if k:
                        pe.wait_ge(v_saved, k)
                    v_project(0, k)
                if job == "K":
                    if k == 0:
                        pe.wait_ge(ctx_loaded[1], 16)
                    pe.wait_ge(k_low_saved, k + 1)
                    k_project(1, 1, k, score_ps[:, k, :])
            transpose_max(3)
            pe.wait_ge(nm_rows, 2)
            pe.wait_ge(kx_ones, 1)
            pe.wait_ge(k_low_saved, 2 * NCH)
            scores(0, 0)
            scores(0, 1)

            def body(i, par, keys_next=True, next_batch=True):
                b = batch(i, par)
                i1, par1 = nxt(i, par, 1)

                def one_chunk(chunks):
                    if not chunks:
                        return
                    n = chunks.pop(0)
                    if n == 0:
                        pe.wait_ge(qx_ready, b + 2)
                    if n == NB - 1:
                        pe.wait_ge(den_taken, b + 1)
                    first = keys_of(n)
                    if first is not None:
                        moved, _ = counts(pe, MOVES * (i1 + 1), MN * (b + 1) + n - NB + 1 if n >= NB else 0)
                        pe.wait_ge(kx_loaded[par1][first[0]][first[1]], moved)
                    max_scores(b + 1, par1, n)

                for t in range(KT):
                    chunks = list(MAX_STEPS[t]) if next_batch else []
                    if next_batch and t == TR_STEP:
                        transpose_max(3 * (b + 2))
                    for h in range(2):
                        if h:
                            pe.wait_ge(exp_done, NHS * b + 2 * t + 1)
                        if t < KT - 1:
                            scores(par, 2 * t + 2 + h)
                        elif next_batch:
                            pe.wait_ge(nm_rows, 2 * (b + 1) + h + 1)
                            scores(par1, h)
                        one_chunk(chunks)
                    job, n = JOBS.get(t, (None, None))
                    if job == "V" and next_batch:
                        if keys_next or n == 0:
                            pe.wait_ge(k_saved, 2 * (NCH * (b + 2) + n))
                        else:
                            pe.wait_ge(v_saved, 3 * (b + 1) + n)
                        v_project(par1, n)
                    if job == "K" and keys_next:
                        loaded, taken = counts(pe, 16 * (i + 2), 3 * (b + 1) + n + 1)
                        if n == 0:
                            pe.wait_ge(ctx_loaded[par], loaded)
                        pe.wait_ge(v_saved, taken)
                        if t < KT - 1:
                            k_project(b + 2, par, n, misc_ps)
                    one_chunk(chunks)
                    pe.wait_ge(exp_done, NHS * b + 2 * t + 2)
                    attend(par, t, 0)
                    last = attend(par, t, 1)
                    one_chunk(chunks)
                last.then_inc(pv_done, 1)
                if keys_next and JOBS.get(KT - 1, (None, 0))[0] == "K":
                    k_project(b + 2, par, NCH - 1, misc_ps)
                saved, taken = counts(pe, b + 1, MN * (b + 2))
                pe.wait_ge(o_saved, saved)
                if next_batch:
                    pe.wait_ge(max_taken, taken)
                nc.tensor.matmul(max_ps[:, 2, 0:2 * PC], den_sel[:, :], o_sb[:, :], start=True, stop=True
                                 ).then_inc(den_done, 1)

            with pe.Fori(0, B // 2 - 1) as i:
                body(i, 0)
                body(i, 1)
            body(3, 0, keys_next=False)
            body(3, 1, keys_next=False, next_batch=False)

            pe.wait_ge(wo_loaded, 16 * H)
            pe.wait_ge(exp_done, NHS * B)
            pe.wait_ge(o_norm_ready, B + 1)
            for r in range(NR):
                for s in range(2):
                    for i in range(2):
                        last = nc.tensor.matmul(token_banks[r][0:RT, 0:D], o_norm[:, r, 2 * s + i, :, :].rearrange("p b c -> p (b c)"),
                                                wo_sb[:, 2 * s + i, :], start=(s + i == 0), stop=(s + i == 2))
                last.then_inc(wo_done, 1)
            for r in range(NR):
                pe.wait_ge(xn_ready, NR + r + 1)
                last = nc.tensor.matmul(misc_ps[:, RT * r:RT * r + RT], xn[:, r, :], ident[0:RT, 0:RT],
                                        start=True, stop=True)
            last.then_inc(xT_done, 1)
            pe.wait_ge(xT_saved, 2)
            pe.wait_ge(ffn_loaded, 16 * (1 + 2 * E))
            for r in range(NR):
                nc.tensor.matmul(max_ps[0:RT, 0, E * r:E * r + E], xnT[:, RT * r:RT * r + RT], gw_sb[:, :],
                                 start=True, stop=True).then_inc(logits_done, 1)

            def gate(n):
                e, j = n // FT, n % FT
                if n >= 2:
                    pe.wait_ge(gelu_ready, n - 1)
                nc.tensor.matmul(gate_banks[n % 2][:, 0:TOK], gu_sb[:, e, 128 * j:128 * j + 128], xnT[:, :],
                                 start=True, stop=True).then_inc(gate_done, 1)

            def up(n):
                e, j = n // FT, n % FT
                pe.wait_ge(xe_ready, e + 1)
                if n >= 2:
                    pe.wait_ge(hact_ready, n - 1)
                nc.tensor.matmul(up_banks[n % 2][:, 0:TOK], gu_sb[:, e, F + 128 * j:F + 128 * j + 128],
                                 x_expert[:, e % 2, :], start=True, stop=True).then_inc(up_done, 1)

            def spread_weight(e):
                if e >= 2:
                    pe.wait_ge(xe_ready, e - 1)
                nc.tensor.matmul(max_ps[:, e % 2, 0:TOK], expert_sel[:, e, :], combT, start=True, stop=True
                                 ).then_inc(bc_done, 1)

            def down(n):
                pe.wait_ge(hact_ready, n + 1)
                nc.tensor.matmul(o_ps[:, 0:TOK], dn_sb[:, n // FT, n % FT, :], hact[:, n % 2, :],
                                 start=(n == 0), stop=(n == E * FT - 1)).then_inc(down_done, 1)

            gate(0)
            gate(1)
            pe.wait_ge(comb_ready, 1)
            for r in range(NR):
                last = nc.tensor.matmul(max_ps[0:16, 2, RT * r:RT * r + RT],
                                        comb_parts[:, r, :, :].bitcast(f32).rearrange("t a e -> t (a e)"),
                                        ident[0:RT, 0:RT], start=True, stop=True)
            last.then_inc(combT_done, 1)
            pe.wait_ge(combT_saved, 1)
            spread_weight(0)
            spread_weight(1)
            for n in range(E * FT):
                up(n)
                if n + 2 < E * FT:
                    gate(n + 2)
                if n >= 1:
                    down(n - 1)
                if n % FT == FT - 1 and n // FT + 2 < E:
                    spread_weight(n // FT + 2)
            down(E * FT - 1)
            pe.wait_ge(y_saved, 1)
            for r in range(NR):
                nc.tensor.matmul(out_banks[r][0:RT, 0:D], yT[:, RT * r:RT * r + RT], ident[:, :],
                                 start=True, stop=True).then_inc(yT_done, 1)


JOBS = {0: ("V", 0), 2: ("K", 0), 4: ("V", 1), 6: ("K", 1), 9: ("V", 2), KT - 1: ("K", 2)}
MAX_STEPS = [[0, 1, 2], [3, 4], [5, 6, 7], [8, 9], [10, 11, 12], [13, 14, 15], [16, 17, 18], [19, 20, 21], [22, 23], [], [], []]
NM_STEP = 8
TR_STEP = 10
FIRST_SPLITS = [5, 8, 18]
FIRST_JOBS = {-2: ("V", 0), -1: ("K", 0), 1: ("V", 1), 5: ("K", 1), 9: ("V", 2), 13: ("K", 2)}


def kernel(x, ctx_1024, g_xattn, g_ffn, L0_xattn_w_q, L0_xattn_w_k, L0_xattn_w_v, L0_xattn_w_o,
           L0_ffn_gate_w, L0_ffn_gate_up_w, L0_ffn_down_w):
    import numpy as np
    import concourse.bacc as bacc
    from concourse.bass_utils import run_bass_kernel_spmd

    layout = np.ascontiguousarray
    arrays = {
        "x": layout(np.asarray(x).reshape(NR, RT, D).transpose(1, 0, 2)),
        "ctxT": layout(np.asarray(ctx_1024).transpose(0, 2, 1)),
        "g_attn": np.asarray(g_xattn),
        "g_ffn": np.asarray(g_ffn),
        "wqT": layout(np.tile(np.asarray(L0_xattn_w_q).T.reshape(D, G, 1, 32), (1, 1, 3, 1)).reshape(D, G, MR)),
        "wkT": layout(np.asarray(L0_xattn_w_k).T),
        "wvT": layout(np.asarray(L0_xattn_w_v).T),
        "woT": layout(np.asarray(L0_xattn_w_o).T),
        "gwT": layout(np.asarray(L0_ffn_gate_w).T),
        "guT": layout(np.asarray(L0_ffn_gate_up_w).transpose(2, 0, 1)),
        "dnT": layout(np.asarray(L0_ffn_down_w).reshape(E, D, FT, 128).transpose(3, 0, 2, 1)),
    }
    nc = bacc.Bacc("TRN2", target_bir_lowering=False, num_devices=1)
    f32 = mybir.dt.float32
    args = [nc.dram_tensor(f"in_{n}", a.shape, f32, kind="ExternalInput").ap() for n, a in arrays.items()]
    result = nc.dram_tensor("out_0", (RT, NR, D), f32, kind="ExternalOutput").ap()
    flamingo_block(nc, *args, result)
    ran = run_bass_kernel_spmd(nc, [{f"in_{n}": a for n, a in arrays.items()}], core_ids=[0])
    return ran.results[0]["out_0"].transpose(1, 0, 2).reshape(B, TQ, D)
```

```python
from contextlib import ExitStack

import concourse.bass as bass
from concourse import mybir

B, TQ, D = 8, 56, 128
TK = 1500
H, HD = 16, 8
E, F = 8, 512
EPS = 1e-5
SCALE = HD ** -0.5

TOK = B * TQ
NR = 4
RT = TOK // NR
KT = -(-TK // 128)
LAST = TK - 128 * (KT - 1)
KPAD = 128 * KT
NCH = 3
CK = 512
HT = 8
HALF = [(0, 128 * HT), (128 * HT, TK - 128 * HT)]
G, GC = 4, 4 * TQ
NP, PC = 8, 2 * TQ
SC = H * TQ
VP = 17
VW = VP * (NP - 1) + 32
MR = 96
KR = 112
MOVES = 16 * 6
NB = 3
NHS = 2 * KT
MN = NCH * NP
FT = F // 128
OWN = (NR - 1) * RT


def chunk(n):
    return CK * n, min(CK, TK - CK * n)


def max_product(n):
    return (n // 2, n % 2) if n < 2 * NP else (n - 2 * NP, 2)


def keys_of(n):
    return {0: (0, 0), NP: (0, 1), 2 * NP: (1, 0), 2 * NP + NP // 2: (1, 1)}.get(n)


def flamingo_block(nc, x, ctxT, g_attn, g_ffn, wqT, wkT, wvT, woT, gwT, guT, dnT, out):
    f32, f32r = mybir.dt.float32, mybir.dt.float32r
    ALU, ACT, AX = mybir.AluOpType, mybir.ActivationFunctionType, mybir.AxisListType

    with ExitStack() as stack:
        def sb(name, shape, dt=f32):
            return stack.enter_context(nc.sbuf_tensor(name, shape, dt))

        def pb(name, shape):
            return stack.enter_context(nc.psum_tensor(name, shape, f32))

        def sem(name):
            return stack.enter_context(nc.semaphore(name))

        kx = sb("kx", [128, 2, G, KPAD], f32r)
        qx = sb("qx", [128, 2, G, GC], f32r)
        q_parts = sb("q_parts", [MR, G, TOK], f32r)
        k_high = sb("k_high", [128, KPAD], f32r)
        k_low = sb("k_low", [128, KPAD], f32r)
        k_full = sb("k_full", [128, KPAD])
        ctx_sb = sb("ctx_sb", [128, 2, KPAD])
        v_sb = sb("v_sb", [128, 2, KT, VW])
        probs = sb("probs", [128, 2, SC])
        o_sb = sb("o_sb", [128, 2 * PC])
        o_norm = sb("o_norm", [128, NR, 4, 2, TQ])
        inv_den = sb("inv_den", [128, 2 * PC])
        part_max = sb("part_max", [PC, NP, NCH])
        neg_max = sb("neg_max", [PC, NP])
        neg_max_parts = sb("neg_max_parts", [PC, 2, NP], f32r)
        wq_sb, wk_sb, wv_sb = sb("wq_sb", [D, G, MR]), sb("wk_sb", [D, D]), sb("wv_sb", [D, D])
        wo_sb = sb("wo_sb", [128, 4, D])
        gw_sb = sb("gw_sb", [D, E])
        gu_sb = sb("gu_sb", [D, E, 2 * F])
        dn_sb = sb("dn_sb", [128, E, FT, D])
        x_sb = sb("x_sb", [RT, NR, D])
        xn = sb("xn", [RT, NR, D])
        xnT = sb("xnT", [D, TOK])
        x1 = sb("x1", [RT, NR, D])
        stats = sb("stats", [RT, NR, 6])
        mean_var = sb("mean_var", [RT, NR, 2])
        var_eps = sb("var_eps", [RT, NR])
        rstd = sb("rstd", [RT, NR])
        minus_half = sb("minus_half", [RT, NR])
        gates = sb("gates", [128, 2])
        tanh_g = sb("tanh_g", [128, 2])
        ident = sb("ident", [128, 128])
        head_mask3 = sb("head_mask3", [128, G, 4])
        head_mask = sb("head_mask", [128, 4])
        den_sel = sb("den_sel", [128, 128])
        row_mask = sb("row_mask", [16, NP])
        expert_sel = sb("expert_sel", [16, E, 128], f32r)
        expert_now = sb("expert_now", [16, 2, 128], f32r)
        before = sb("before", [RT, E, E])
        logits = sb("logits", [RT, NR, E])
        row8 = sb("row8", [RT, 4, NR])
        pr = sb("pr", [RT, NR, E])
        rank = sb("rank", [RT, NR, E])
        comb = sb("comb", [RT, NR, E])
        comb_parts = sb("comb_parts", [RT, NR, 2, E], f32r)
        combT = q_parts[0:16, 0, :]
        out_sb = xn
        o_flat = o_norm[:, :, :, :, :].rearrange("p r s b c -> p (r s b c)")
        greater = ctx_sb[0:RT, 0, 0:NR * E * E].rearrange("t (r e j) -> t r e j", r=NR, e=E)
        equal = ctx_sb[0:RT, 1, 0:NR * E * E].rearrange("t (r e j) -> t r e j", r=NR, e=E)
        kx_flat = kx[:, :, :, :].rearrange("p a g k -> p (a g k)")
        weight_parts = kx_flat[:, 0:3 * 4 * F].rearrange("p (w a s f) -> p w a s f", w=3, a=2, s=2)
        GATE, UP, DOWN = range(3)
        hact_parts = kx_flat[:, 12 * F:12 * F + 2 * FT * TOK].rearrange("p (j s t) -> p j s t", j=FT, s=2)
        x_high = kx_flat[:, 12 * F + 2 * FT * TOK:12 * F + (2 * FT + 1) * TOK]
        x_low = kx_flat[:, 12 * F + (2 * FT + 1) * TOK:12 * F + (2 * FT + 2) * TOK]
        x_expert_high = k_high[:, 0:2 * TOK].rearrange("p (a t) -> p a t", a=2)
        x_expert_low = k_low[:, 0:2 * TOK].rearrange("p (a t) -> p a t", a=2)
        zeros = k_high[:, 2 * TOK:2 * TOK + 128]
        x_expert = k_full[:, 0:TOK]
        hact = probs[:, :, :].rearrange("p a (b t) -> p (a b) t", b=2)
        gelu_sb = v_sb[:, :, :, :].rearrange("k a t c -> k (a t c)")[:, 0:2 * FT * TOK].rearrange(
            "p (a j t) -> p a j t", a=2, j=FT)
        yT = o_flat[:, 2 * TOK:3 * TOK]

        score_ps = pb("score_ps", [128, NB, 512])
        max_ps = pb("max_ps", [128, NB, 512])
        o_ps = pb("o_ps", [128, 512])
        misc_ps = pb("misc_ps", [128, 512])
        q_banks = [max_ps[:, 0, :], max_ps[:, 1, :], max_ps[:, 2, :], o_ps[:, :]]
        token_banks = [max_ps[:, 0, D * r:D * r + D] for r in range(NR - 1)] + [o_ps[:, 0:D]]
        gate_banks = [score_ps[:, 0, :], score_ps[:, 1, :]]
        up_banks = [score_ps[:, 2, :], misc_ps[:, :], max_ps[:, 2, :]]
        out_banks = gate_banks + up_banks[0:2]

        x_loaded, w_loaded, wo_loaded, ffn_loaded, g_loaded = map(sem, ("x_loaded", "w_loaded", "wo_loaded", "ffn_loaded", "g_loaded"))
        ctx_begun = sem("ctx_begun")
        ctx_loaded = [sem("ctx_loaded0"), sem("ctx_loaded1")]
        kx_loaded = [[[sem(f"kx_loaded{p}{h}{g}") for g in range(2)] for h in range(2)] for p in range(2)]
        consts, mask_ready, select_all, cleared, wo_cleared, pool_step = map(sem, ("consts", "mask_ready", "select_all", "cleared", "wo_cleared", "pool_step"))
        var_ready, rstd_ready, xn_ready, xT_done, xT_saved = map(sem, ("var_ready", "rstd_ready", "xn_ready", "xT_done", "xT_saved"))
        q_done, q_high_saved, q_low_saved = map(sem, ("q_done", "q_high_saved", "q_low_saved"))
        k_done, k_saved, k_low_saved = map(sem, ("k_done", "k_saved", "k_low_saved"))
        v_done, v_saved = map(sem, ("v_done", "v_saved"))
        kx_ones, qx_ready = sem("kx_ones"), sem("qx_ready")
        scores_done, exp_done, pv_done = map(sem, ("scores_done", "exp_done", "pv_done"))
        max_done, max_taken = map(sem, ("max_done", "max_taken"))
        nm_step, nmT_done, nm_rows = map(sem, ("nm_step", "nmT_done", "nm_rows"))
        o_saved, den_done, den_taken, o_norm_ready = map(sem, ("o_saved", "den_done", "den_taken", "o_norm_ready"))
        ln_step, tanh_ready = map(sem, ("ln_step", "tanh_ready"))
        wo_done, x1_ready = map(sem, ("wo_done", "x1_ready"))
        logits_done, logits_exp, router_step, comb_ready = map(sem, ("logits_done", "logits_exp", "router_step", "comb_ready"))
        combT_done, combT_saved = map(sem, ("combT_done", "combT_saved"))
        select_ready, bc_done, xe_full, xe_high, xe_ready, x_split = map(sem, ("select_ready", "bc_done", "xe_full", "xe_high", "xe_ready", "x_split"))
        weights_high, weights_low, zeros_ready = map(sem, ("weights_high", "weights_low", "zeros_ready"))
        gate_done, up_done, gelu_ready, hact_full, hact_high, hact_ready, down_done = map(
            sem, ("gate_done", "up_done", "gelu_ready", "hact_full", "hact_high", "hact_ready", "down_done"))
        y_saved, yT_done, out_ready, stored = map(sem, ("y_saved", "yT_done", "out_ready", "stored"))

        block = stack.enter_context(nc.Block())

        def bc(ap, shape):
            return ap.to_broadcast(shape)

        def nxt(i, par, k):
            return i + (par + k) // 2, (par + k) % 2

        def batch(i, par):
            return 2 * i + par

        def counts(eng, *values):
            for v in values:
                if not isinstance(v, int):
                    eng.lower_val(v)
            return values

        def weights_of(kind, e):
            return [gu_sb[:, e, 0:F], gu_sb[:, e, F:2 * F], dn_sb[:, e, :, :].rearrange("p j d -> p (j d)")][kind]

        def block_diagonal(eng, b, par):
            src = q_parts[:, :, bass.ds(TQ * b, TQ)].bitcast(f32).unsqueeze(2)
            mask = head_mask[0:MR, :].unsqueeze(1).unsqueeze(3)
            return eng.tensor_tensor(qx[0:MR, par, :, :].rearrange("p g (h c) -> p g h c", h=4),
                                     bc(src, [MR, G, 4, TQ]), bc(mask, [MR, G, 4, TQ]), ALU.mult)

        @block.sync
        def _(sp):
            def move_keys(par, part):
                start, size = HALF[part]
                for g in range(G):
                    for row, src in ((0, k_high), (1, k_low), (2, k_high)):
                        sp.dma_start(kx[32 * row:32 * row + 32, par, g, start:start + size].bitcast(f32),
                                     src[32 * g:32 * g + 32, start:start + size].bitcast(f32)
                                     ).then_inc(kx_loaded[par][part][g // 2], 16)

            sp.dma_start(x_sb[:, :, :], x).then_inc(x_loaded, 16)
            sp.dma_start(wk_sb[:, :], wkT).then_inc(w_loaded, 16)
            sp.dma_start(ctx_sb[:, 0, 0:2 * CK], ctxT[0][:, 0:2 * CK]).then_inc(ctx_begun, 16)
            sp.dma_start(ctx_sb[:, 0, 2 * CK:TK], ctxT[0][:, 2 * CK:TK]).then_inc(ctx_loaded[0], 16)
            sp.dma_start(ctx_sb[:, 1, 0:TK], ctxT[1]).then_inc(ctx_loaded[1], 16)
            for half in range(2):
                sp.wait_ge(k_low_saved, 2 + half)
                move_keys(0, half)
            sp.wait_ge(k_low_saved, NCH + 2)
            move_keys(1, 0)
            sp.wait_ge(v_done, 3)
            sp.dma_start(ctx_sb[:, 0, 0:TK], ctxT[2]).then_inc(ctx_loaded[0], 16)
            def body(i, par, ctx_next=True, keys_next=True):
                b = batch(i, par)
                par1 = 1 - par
                split_2, split_1, left_2, left_1, taken = counts(
                    sp, NCH * (b + 2), NCH * (b + 2) + 2, NHS * b + 1, NHS * b + 2 * HT, 3 * (b + 2))
                sp.wait_ge(k_low_saved, split_2)
                sp.wait_ge(scores_done, left_2)
                move_keys(par1, 1)
                if keys_next:
                    sp.wait_ge(k_low_saved, split_1)
                    sp.wait_ge(scores_done, left_1)
                    move_keys(par, 0)
                if ctx_next:
                    sp.wait_ge(v_done, taken)
                    sp.dma_start(ctx_sb[:, par1, 0:TK], ctxT[b + 3]).then_inc(ctx_loaded[par1], 16)
                load_expert(b)

            def load_expert(e):
                sp.dma_start(gu_sb[:, e, :], guT[:, e, :]).then_inc(ffn_loaded, 16)
                sp.dma_start(dn_sb[:, e, :, :], dnT[:, e, :, :]).then_inc(ffn_loaded, 16)

            with sp.Fori(0, 2) as i:
                body(i, 0)
                body(i, 1)
            body(2, 0)
            body(2, 1, ctx_next=False)
            body(3, 0, ctx_next=False, keys_next=False)
            for e in range(B - 1, E):
                load_expert(e)
            sp.wait_ge(out_ready, NR)
            sp.dma_start(out, out_sb[:, :, :]).then_inc(stored, 16)
            sp.wait_ge(stored, 16)

        @block.gpsimd
        def _(pool):
            steps = [0]

            def serial(ins):
                steps[0] += 1
                ins.then_inc(pool_step, 1)
                pool.wait_ge(pool_step, steps[0])

            serial(nc.gpsimd.memset(minus_half[:, :], -0.5))
            serial(nc.gpsimd.memset(ident[:, :], 0.0))
            serial(nc.gpsimd.affine_select(out=ident[:, :], in_=ident[:, :], compare_op=ALU.not_equal, fill=1.0,
                                           base=0, pattern=[[-1, 128]], channel_multiplier=1))
            serial(nc.gpsimd.memset(head_mask3[:, :, :], 1.0))
            serial(nc.gpsimd.affine_select(out=head_mask3[:, :, :], in_=head_mask3[:, :, :], compare_op=ALU.is_ge,
                                           fill=0.0, base=0, pattern=[[-32, G], [-HD, 4]], channel_multiplier=1))
            serial(nc.gpsimd.affine_select(out=head_mask3[:, :, :], in_=head_mask3[:, :, :], compare_op=ALU.is_ge,
                                           fill=0.0, base=HD - 1, pattern=[[32, G], [HD, 4]], channel_multiplier=-1))
            serial(nc.gpsimd.memset(row_mask[:, :], 0.0))
            for r in (0, NP):
                serial(nc.gpsimd.affine_select(out=row_mask[:, :], in_=row_mask[:, :], compare_op=ALU.not_equal,
                                               fill=1.0, base=-r, pattern=[[-1, NP]], channel_multiplier=1))
            serial(nc.gpsimd.memset(den_sel[:, :], 0.0))
            sel = den_sel[:, :].rearrange("k (j m) -> k j m", j=4)
            serial(nc.gpsimd.affine_select(out=sel, in_=sel, compare_op=ALU.not_equal, fill=1.0,
                                           base=-16, pattern=[[-32, 4], [0, 32]], channel_multiplier=1))
            serial(nc.gpsimd.memset(before[:, :, :], 1.0))
            nc.gpsimd.affine_select(out=before[:, :, :], in_=before[:, :, :], compare_op=ALU.is_ge, fill=0.0,
                                    base=-1, pattern=[[1, E], [-1, E]], channel_multiplier=0).then_inc(consts, 1)
            pool.wait_ge(consts, 1)
            pool.wait_ge(var_ready, 1)
            nc.gpsimd.tensor_tensor(rstd[:, :], var_eps[:, :], minus_half[:, :], ALU.pow).then_inc(rstd_ready, 1)

            def stage(b, par):
                block_diagonal(nc.gpsimd, b, par).then_inc(qx_ready, 1)

            def k_rest(b, n, part=None, move_count=0):
                start, size = chunk(n)
                saved, move_count = counts(pool, 2 * (NCH * b + n + 1), move_count)
                pool.wait_ge(k_saved, saved)
                nc.gpsimd.tensor_tensor(k_low[:, start:start + size], k_full[:, start:start + size],
                                        k_high[:, start:start + size].bitcast(f32), ALU.subtract
                                        ).then_inc(k_low_saved, 1)

            pool.wait_ge(rstd_ready, 1)
            nc.gpsimd.memset(kx[MR:128, :, :, :].bitcast(f32), 1.0).then_inc(kx_ones, 1)
            pool.wait_ge(kx_ones, 1)
            pool.wait_ge(mask_ready, 1)
            pool.wait_ge(q_low_saved, G)
            pool.wait_ge(qx_ready, 1)
            stage(1, 1)
            pool.wait_ge(wo_cleared, 1)
            for s in range(2):
                for i in range(2):
                    for j in range(4):
                        h = 2 * (4 * s + j) + i
                        r = 32 * j + HD * i
                        pool.dma_start(wo_sb[r:r + HD, 2 * s + i, :], woT[HD * h:HD * h + HD, :]).then_inc(wo_loaded, 16)

            def body(i, par):
                b = batch(i, par)
                for n in range(NCH):
                    if n == NCH - 1:
                        staged, left = counts(pool, b + 2, NHS * (b + 1))
                        pool.wait_ge(qx_ready, staged)
                        pool.wait_ge(scores_done, left)
                        stage(b + 2, par)
                    k_rest(b + 2, n)
                normalise(i, par)

            def normalise(i, par):
                four = "p (s c) -> p s c"
                pool.wait_ge(den_taken, batch(i, par) + 2)
                nc.gpsimd.tensor_tensor(o_norm[:, i, :, par, :], o_sb[:, :].rearrange(four, s=4),
                                        inv_den[:, :].rearrange(four, s=4), ALU.mult).then_inc(o_norm_ready, 1)

            with pool.Fori(0, B // 2 - 1) as i:
                body(i, 0)
                body(i, 1)
            normalise(3, 0)
            def weights_rest(kind, e, par, made):
                pool.wait_ge(weights_high, made)
                nc.gpsimd.tensor_tensor(weight_parts[:, kind, par, 1, :], weights_of(kind, e),
                                        weight_parts[:, kind, par, 0, :].bitcast(f32), ALU.subtract
                                        ).then_inc(weights_low, 1)

            def select(e, par):
                nc.gpsimd.tensor_copy(expert_now[:, par, :], expert_sel[:, e, :].bitcast(f32)).then_inc(select_ready, 1)

            pool.wait_ge(qx_ready, B)
            pool.wait_ge(var_ready, 2)
            nc.gpsimd.tensor_tensor(rstd[:, 0:NR - 1], var_eps[:, 0:NR - 1], minus_half[:, 0:NR - 1], ALU.pow
                                    ).then_inc(rstd_ready, 1)
            for made, (kind, e) in enumerate(FIRST_WEIGHTS[:-1]):
                if made == 2:
                    normalise(3, 1)
                weights_rest(kind, e, e % 2, made + 1)
            pool.wait_ge(select_all, 1)
            select(0, 0)
            pool.wait_ge(var_ready, 3)
            nc.gpsimd.tensor_tensor(rstd[:, NR - 1:NR], var_eps[:, NR - 1:NR], minus_half[:, NR - 1:NR], ALU.pow
                                    ).then_inc(rstd_ready, 1)
            weights_rest(GATE, 2, 0, len(FIRST_WEIGHTS))

            def expert(i, par, split_gate=True):
                e = batch(i, par)
                pool.wait_ge(up_done, FT * e + 1)
                select(e + 1, 1 - par)
                made = 3 * e + 5 if split_gate else 2 * e + 10
                weights_rest(UP, e + 1, 1 - par, made + 1)
                weights_rest(DOWN, e + 1, 1 - par, made + 2)
                if split_gate:
                    weights_rest(GATE, e + 3, 1 - par, made + 3)

            with pool.Fori(0, 2) as i:
                expert(i, 0)
                expert(i, 1)
            expert(2, 0)
            expert(2, 1, split_gate=False)
            expert(3, 0, split_gate=False)

        @block.scalar
        def _(act):
            act.dma_start(wq_sb[:, :, :], wqT).then_inc(w_loaded, 16)
            act.dma_start(wv_sb[:, :], wvT).then_inc(w_loaded, 16)
            act.dma_start(gates[:, 0:1], g_attn.partition_broadcast(128)).then_inc(g_loaded, 16)
            act.dma_start(gates[:, 1:2], g_ffn.partition_broadcast(128)).then_inc(g_loaded, 16)
            act.dma_start(gw_sb[:, :], gwT).then_inc(ffn_loaded, 16)
            act.wait_ge(g_loaded, 32)
            nc.scalar.activation(tanh_g[:, :], gates[:, :], ACT.Tanh).then_inc(tanh_ready, 1)

            def k_copy(b, n, bank, par=None, move_count=0, whole=True):
                start, size = chunk(n)
                projected, move_count = counts(act, NCH * b + n + 1, move_count)
                if par is not None and n != 1:
                    act.wait_ge(kx_loaded[par][n // 2][0], move_count)
                    act.wait_ge(kx_loaded[par][n // 2][1], move_count)
                act.wait_ge(k_done, projected)
                nc.scalar.activation(k_high[:, start:start + size], bank[:, 0:size], ACT.Copy
                                     ).then_inc(k_saved, 1 if whole else 2)
                if whole:
                    nc.scalar.activation(k_full[:, start:start + size], bank[:, 0:size], ACT.Copy).then_inc(k_saved, 1)

            def v_copy(b, par, n):
                act.wait_ge(v_done, 3 * b + n + 1)
                dst = v_sb[:, par, 4 * n:4 * n + 4, 0:VP * NP].rearrange("k t (p c) -> k t p c", p=NP)[:, :, :, 0:16]
                src = misc_ps[:, :].rearrange("k (t p c) -> k t p c", t=4, p=NP)
                nc.scalar.activation(dst, src, ACT.Copy).then_inc(v_saved, 1)

            def exp_half(b, hs):
                t, h = hs // 2, hs % 2
                act.wait_ge(scores_done, NHS * b + hs + 1)
                m = 128 if t < KT - 1 else LAST
                nc.scalar.activation(probs[0:m, t % 2, SC // 2 * h:SC // 2 * (h + 1)], score_ps[0:m, hs % NB, 0:SC // 2],
                                     ACT.Exp, scale=SCALE).then_inc(exp_done, 1)

            k_copy(0, 0, score_ps[:, 0, :], whole=False)
            k_copy(0, 1, score_ps[:, 1, :], whole=False)
            act.wait_ge(xT_done, 1)
            nc.scalar.activation(xnT[:, :], misc_ps[:, 0:TOK], ACT.Copy).then_inc(xT_saved, 1)
            k_copy(0, 2, score_ps[:, 2, :], whole=False)
            for g in range(G):
                act.wait_ge(q_done, g + 1)
                nc.scalar.activation(q_parts[:, g, :], q_banks[g][0:MR, 0:TOK], ACT.Copy).then_inc(q_high_saved, 1)
            act.wait_ge(cleared, 2)
            for n in range(NCH):
                v_copy(0, 0, n)
                k_copy(1, n, score_ps[:, n, :], 0, MOVES, whole=False)
            exp_half(0, 0)
            exp_half(0, 1)

            def body(i, par, keys_next=True, next_batch=True):
                b = batch(i, par)
                i1, par1 = nxt(i, par, 1)
                for t in range(KT):
                    for h in range(2):
                        if t < KT - 1:
                            exp_half(b, 2 * t + 2 + h)
                        elif next_batch:
                            exp_half(b + 1, h)
                    if not next_batch and t == TOKEN_STEPS[1]:
                        act.wait_ge(xT_done, 2)
                        nc.scalar.activation(xnT[:, 0:OWN], misc_ps[:, 0:OWN], ACT.Copy).then_inc(xT_saved, 1)
                    job, n = JOBS.get(t, (None, None))
                    if next_batch and job == "V":
                        v_copy(b + 1, par1, n)
                    if keys_next and job == "K":
                        k_copy(b + 2, n, misc_ps, par1, MOVES * (i1 + 1))

            with act.Fori(0, B // 2 - 1) as i:
                body(i, 0)
                body(i, 1)
            body(3, 0, keys_next=False)
            body(3, 1, keys_next=False, next_batch=False)

            def weights_copy(kind, e, par):
                nc.scalar.activation(weight_parts[:, kind, par, 0, :], weights_of(kind, e), ACT.Copy).then_inc(weights_high, 1)

            def gelu(e, par, j):
                act.wait_ge(gate_done, FT * e + j + 1)
                nc.scalar.activation(gelu_sb[:, par, j, :], gate_banks[j % 2][:, 0:TOK], ACT.Gelu).then_inc(gelu_ready, 1)

            act.wait_ge(ffn_loaded, 16 * (1 + 2 * E))
            act.wait_ge(scores_done, NHS * B)
            for kind, e in FIRST_WEIGHTS[:-1]:
                weights_copy(kind, e, e % 2)
            act.wait_ge(xT_done, 3)
            nc.scalar.activation(xnT[:, OWN:TOK], misc_ps[:, OWN:TOK], ACT.Copy).then_inc(xT_saved, 1)
            nc.scalar.activation(x_high, misc_ps[:, 0:TOK], ACT.Copy).then_inc(xT_saved, 1)
            act.wait_ge(router_step, 2)
            nc.scalar.activation(pr[:, :, :], logits[:, :, :], ACT.Exp).then_inc(logits_exp, 1)
            act.wait_ge(pv_done, B)
            for n in range(2 * FT):
                if n == FT:
                    weights_copy(GATE, 2, 0)
                if n == 2 * FT - 2:
                    act.wait_ge(combT_done, 1)
                    nc.scalar.activation(combT, max_ps[0:16, 2, 0:TOK], ACT.Copy).then_inc(combT_saved, 1)
                gelu(n // FT, n // FT, n % FT)

            def expert(i, par, split_gate=True, gates=True, more=True):
                e = batch(i, par)

                def next_gelu(j):
                    if gates:
                        gelu(e + 2, par, j)

                for j in range(FT):
                    act.wait_ge(hact_full, FT * e + j + 1)
                    nc.scalar.activation(hact_parts[:, j, 0, :], hact[:, j, :], ACT.Copy).then_inc(hact_high, 1)
                    if j == 1:
                        next_gelu(0)
                if more:
                    weights_copy(UP, e + 1, 1 - par)
                next_gelu(1)
                if more:
                    weights_copy(DOWN, e + 1, 1 - par)
                next_gelu(2)
                if split_gate:
                    weights_copy(GATE, e + 3, 1 - par)
                next_gelu(3)

            with act.Fori(0, 2) as i:
                expert(i, 0)
                expert(i, 1)
            expert(2, 0)
            expert(2, 1, split_gate=False)
            expert(3, 0, split_gate=False, gates=False)
            expert(3, 1, split_gate=False, gates=False, more=False)
            act.wait_ge(down_done, E * FT)
            nc.scalar.activation(yT, o_ps[:, 0:TOK], ACT.Copy).then_inc(y_saved, 1)

        @block.vector
        def _(dve):
            ln = [0]

            def layer_norm(src, turn, first, end):
                for r in range(first, end):
                    nc.vector.bn_stats(stats[:, r, :], src[:, r, :]).then_inc(ln_step, 1)
                    ln[0] += 1
                dve.wait_ge(ln_step, ln[0])
                for r in range(first, end):
                    nc.vector.bn_aggr(mean_var[:, r, :], stats[:, r, :]).then_inc(ln_step, 1)
                    ln[0] += 1
                dve.wait_ge(ln_step, ln[0])
                nc.vector.tensor_scalar(var_eps[:, first:end], mean_var[:, first:end, 1], EPS, None, ALU.add
                                        ).then_inc(var_ready, 1)
                dve.wait_ge(rstd_ready, turn)
                for r in range(first, end):
                    nc.vector.tensor_scalar(xn[:, r, :], src[:, r, :], mean_var[:, r, 0:1], rstd[:, r:r + 1],
                                            ALU.subtract, ALU.mult).then_inc(xn_ready, 1)

            def attended(turn, first, end):
                for r in range(first, end):
                    dve.wait_ge(wo_done, turn - 1)
                    nc.vector.scalar_tensor_tensor(x1[:, r, :], token_banks[r][0:RT, :], tanh_g[0:RT, 0:1],
                                                   x_sb[:, r, :], ALU.mult, ALU.add).then_inc(x1_ready, 1)
                dve.wait_ge(x1_ready, end)
                layer_norm(x1, turn, first, end)

            def k_rest(b, n, bank):
                start, size = chunk(n)
                dve.wait_ge(k_saved, 2 * (NCH * b + n + 1))
                nc.vector.tensor_tensor(k_low[:, start:start + size], bank[:, 0:size],
                                        k_high[:, start:start + size].bitcast(f32), ALU.subtract
                                        ).then_inc(k_low_saved, 1)

            def take_max(b, n):
                p, c = max_product(n)
                size = chunk(c)[1]
                dve.wait_ge(max_done, MN * b + n + 1)
                nc.vector.reduce_max(part_max[:, p, c:c + 1], max_ps[0:PC, n % NB, 0:size],
                                     AX.X).then_inc(max_taken, 1)

            def negate_max(b):
                dve.wait_ge(max_taken, MN * (b + 1))
                nc.vector.tensor_reduce(neg_max[:, :], part_max[:, :, :], AX.X, ALU.max, negate=True).then_inc(nm_step, 1)
                dve.wait_ge(nm_step, 3 * b + 1)
                nc.vector.tensor_copy(neg_max_parts[:, 0, :], neg_max[:, :]).then_inc(nm_step, 1)
                dve.wait_ge(nm_step, 3 * b + 2)
                nc.vector.tensor_tensor(neg_max_parts[:, 1, :], neg_max[:, :], neg_max_parts[:, 0, :].bitcast(f32),
                                        ALU.subtract).then_inc(nm_step, 1)

            def max_rows(b, par):
                dve.wait_ge(nmT_done, b + 1)
                for h in range(2):
                    dst = qx[MR:KR, par, 2 * h:2 * h + 2, :].rearrange("r g (p c) -> r (g p) c", p=2)
                    half = [16, NP // 2, PC]
                    nc.vector.tensor_tensor(dst, bc(max_ps[0:16, 0, 0:PC].unsqueeze(1), half),
                                            bc(row_mask[:, NP // 2 * h:NP // 2 * (h + 1)].unsqueeze(2), half), ALU.mult
                                            ).then_inc(nm_rows, 1)

            nc.vector.memset(ctx_sb[:, 0, TK:KPAD], 0.0).then_inc(o_norm_ready, 1)
            nc.vector.memset(ctx_sb[:, 1, TK:KPAD], 0.0).then_inc(den_taken, 1)
            values = v_sb[:, :, :, 0:VP * NP].rearrange("k a t (p c) -> k (a t) p c", p=NP)
            nc.vector.memset(values[:, :, :, VP - 1:VP], 1.0).then_inc(cleared, 1)
            nc.vector.memset(v_sb[:, :, :, VP * NP:VW], 1.0).then_inc(cleared, 1)
            nc.vector.memset(wo_sb[:, :, :], 0.0).then_inc(wo_cleared, 1)
            dve.wait_ge(x_loaded, 16)
            layer_norm(x_sb, 1, 0, NR)
            dve.wait_ge(consts, 1)
            nc.vector.tensor_copy(expert_sel[:, :, :], bc(row_mask[:, :].unsqueeze(2), [16, E, 128])).then_inc(select_all, 1)
            for n in range(NCH):
                k_rest(0, n, score_ps[:, n, :])
            nc.vector.tensor_reduce(head_mask[:, :], head_mask3[:, :, :].rearrange("p g h -> p h g"), AX.X,
                                    ALU.add).then_inc(mask_ready, 1)
            for g in range(G):
                dve.wait_ge(q_high_saved, g + 1)
                low = q_parts[64:MR, g, :]
                nc.vector.tensor_tensor(low, q_banks[g][64:MR, 0:TOK], low.bitcast(f32),
                                        ALU.subtract).then_inc(q_low_saved, 1)
            dve.wait_ge(mask_ready, 1)
            dve.wait_ge(q_low_saved, G)
            block_diagonal(nc.vector, 0, 0).then_inc(qx_ready, 1)
            for n in range(MN):
                take_max(0, n)
                if n in FIRST_SPLITS:
                    k_rest(1, FIRST_SPLITS.index(n), score_ps[:, FIRST_SPLITS.index(n), :])
            negate_max(0)
            max_rows(0, 0)

            def body(i, par, next_batch=True):
                b = batch(i, par)
                par1 = 1 - par
                for t in range(KT):
                    for n in (MAX_STEPS[t] if next_batch else ()):
                        take_max(b + 1, n)
                    if next_batch and t == NM_STEP:
                        negate_max(b + 1)
                        max_rows(b + 1, par1)
                complete, normalised = counts(dve, b + 1, b + 1)
                dve.wait_ge(o_norm_ready, normalised)
                dve.wait_ge(pv_done, complete)
                nc.vector.tensor_copy(o_sb[:, :], o_ps[:, 0:2 * PC]).then_inc(o_saved, 1)
                dve.wait_ge(den_done, b + 1)
                nc.vector.reciprocal(inv_den[:, :], max_ps[:, 2, 0:2 * PC]).then_inc(den_taken, 1)

            with dve.Fori(0, B // 2 - 1) as i:
                body(i, 0)
                body(i, 1)
            body(3, 0)
            dve.wait_ge(tanh_ready, 1)
            attended(2, 0, NR - 1)
            body(3, 1, next_batch=False)
            attended(3, NR - 1, NR)

            dve.wait_ge(xT_saved, 4)
            nc.vector.tensor_tensor(x_low, xnT[:, :], x_high.bitcast(f32), ALU.subtract).then_inc(x_split, 1)
            nc.vector.memset(zeros.bitcast(f32), 0.0).then_inc(zeros_ready, 1)

            steps = [0]

            def serial(ins):
                steps[0] += 1
                ins.then_inc(router_step, 1)
                dve.wait_ge(router_step, steps[0])

            dve.wait_ge(logits_done, NR)
            raw = max_ps[0:RT, 0, 0:NR * E].rearrange("t (r e) -> t r e", r=NR)
            big = [RT, NR, E]
            serial(nc.vector.reduce_max(row8[:, 0, :], raw, AX.X))
            serial(nc.vector.tensor_tensor(logits[:, :, :], raw, bc(row8[:, 0, :].unsqueeze(2), big), ALU.subtract))
            dve.wait_ge(logits_exp, 1)
            serial(nc.vector.tensor_reduce(row8[:, 1, :], pr[:, :, :], AX.X, ALU.add))
            serial(nc.vector.reciprocal(row8[:, 2, :], row8[:, 1, :]))
            serial(nc.vector.tensor_tensor(pr[:, :, :], pr[:, :, :], bc(row8[:, 2, :].unsqueeze(2), big), ALU.mult))
            cube = [RT, NR, E, E]
            other, own = bc(pr[:, :, :].unsqueeze(2), cube), bc(pr[:, :, :].unsqueeze(3), cube)
            serial(nc.vector.tensor_tensor(equal, other, own, ALU.is_equal))
            serial(nc.vector.tensor_tensor(greater, other, own, ALU.is_gt))
            serial(nc.vector.tensor_tensor(equal, equal, bc(before[:, :, :].unsqueeze(1), cube),
                                           ALU.mult))
            serial(nc.vector.tensor_tensor(greater, greater, equal, ALU.add))
            serial(nc.vector.tensor_reduce(rank[:, :, :], greater, AX.X, ALU.add))
            serial(nc.vector.scalar_tensor_tensor(comb[:, :, :], rank[:, :, :], 1.5, pr[:, :, :], ALU.is_lt, ALU.mult))
            serial(nc.vector.tensor_reduce(row8[:, 3, :], comb[:, :, :], AX.X, ALU.add))
            serial(nc.vector.reciprocal(row8[:, 1, :], row8[:, 3, :]))
            serial(nc.vector.tensor_tensor(comb[:, :, :], comb[:, :, :], bc(row8[:, 1, :].unsqueeze(2), big), ALU.mult))
            serial(nc.vector.tensor_copy(comb_parts[:, :, 0, :], comb[:, :, :]))
            nc.vector.tensor_tensor(comb_parts[:, :, 1, :], comb[:, :, :], comb_parts[:, :, 0, :].bitcast(f32),
                                    ALU.subtract).then_inc(comb_ready, 1)

            def x_expert_full(e, par):
                dve.wait_ge(bc_done, e + 1)
                nc.vector.tensor_tensor(x_expert, max_ps[:, par, 0:TOK], xnT[:, :], ALU.mult).then_inc(xe_full, 1)

            def x_expert_copy(e, par):
                dve.wait_ge(xe_full, e + 1)
                nc.vector.tensor_copy(x_expert_high[:, par, :], x_expert).then_inc(xe_high, 1)

            def x_expert_rest(e, par):
                dve.wait_ge(xe_high, e + 1)
                nc.vector.tensor_tensor(x_expert_low[:, par, :], x_expert, x_expert_high[:, par, :].bitcast(f32),
                                        ALU.subtract).then_inc(xe_ready, 1)

            x_expert_full(0, 0)
            x_expert_copy(0, 0)
            x_expert_rest(0, 0)

            def expert(i, par, more=True):
                e = batch(i, par)

                def product(j):
                    gated, multiplied = counts(dve, FT * e + j + 1, FT * e + j + 1)
                    dve.wait_ge(gelu_ready, gated)
                    dve.wait_ge(up_done, multiplied)
                    nc.vector.tensor_tensor(hact[:, j, :], up_banks[j % NB][:, 0:TOK], gelu_sb[:, par, j, :],
                                            ALU.mult).then_inc(hact_full, 1)

                def rest(j):
                    dve.wait_ge(hact_high, FT * e + j + 1)
                    nc.vector.tensor_tensor(hact_parts[:, j, 1, :], hact[:, j, :],
                                            hact_parts[:, j, 0, :].bitcast(f32), ALU.subtract).then_inc(hact_ready, 1)

                product(0)
                product(1)
                rest(0)
                product(2)
                rest(1)
                product(3)
                if more:
                    x_expert_full(e + 1, 1 - par)
                rest(2)
                if more:
                    x_expert_copy(e + 1, 1 - par)
                rest(3)
                if more:
                    x_expert_rest(e + 1, 1 - par)

            with dve.Fori(0, E // 2 - 1) as i:
                expert(i, 0)
                expert(i, 1)
            expert(E // 2 - 1, 0)
            expert(E // 2 - 1, 1, more=False)
            for r in range(NR):
                dve.wait_ge(yT_done, r + 1)
                nc.vector.scalar_tensor_tensor(out_sb[:, r, :], out_banks[r][0:RT, 0:D], tanh_g[0:RT, 1:2],
                                               x1[:, r, :], ALU.mult, ALU.add).then_inc(out_ready, 1)

        @block.tensor
        def _(pe):
            def k_project(b, par, n, bank):
                start, size = chunk(n)
                nc.tensor.matmul(bank[:, 0:size], wk_sb[:, :], ctx_sb[:, par, start:start + size],
                                 start=True, stop=True).then_inc(k_done, 1)

            def v_project(par, n):
                for k in range(4):
                    t = 4 * n + k
                    last = nc.tensor.matmul(misc_ps[:, 128 * k:128 * k + 128], ctx_sb[:, par, 128 * t:128 * t + 128],
                                            wv_sb[:, :], start=True, stop=True)
                last.then_inc(v_done, 1)

            def scores(par, hs):
                t, h = hs // 2, hs % 2
                m = 128 if t < KT - 1 else LAST
                for g in (2 * h, 2 * h + 1):
                    last = nc.tensor.matmul(score_ps[0:m, hs % NB, GC * (g % 2):GC * (g % 2) + GC],
                                            kx[0:KR, par, g, 128 * t:128 * t + m], qx[0:KR, par, g, :],
                                            start=True, stop=True)
                last.then_inc(scores_done, 1)

            def max_scores(b, par, n):
                p, c = max_product(n)
                start, size = chunk(c)
                if n >= NB:
                    pe.wait_ge(max_taken, MN * b + n - NB + 1)
                nc.tensor.matmul(max_ps[0:PC, n % NB, 0:size], qx[0:MR, par, p // 2, PC * (p % 2):PC * (p % 2) + PC],
                                 kx[0:MR, par, p // 2, start:start + size], start=True, stop=True
                                 ).then_inc(max_done, 1)

            def attend(par, t, s):
                m = 128 if t < KT - 1 else LAST
                for j in range(4):
                    p = 4 * s + j
                    last = nc.tensor.matmul(o_ps[32 * j:32 * j + 32, PC * s:PC * s + PC],
                                            v_sb[0:m, par, t, VP * p:VP * p + 32],
                                            probs[0:m, t % 2, PC * p:PC * p + PC],
                                            start=(t == 0 and s == 0), stop=(t == KT - 1), skip_group_check=True)
                return last

            def transpose_max(ready):
                pe.wait_ge(nm_step, ready)
                nc.tensor.matmul(max_ps[0:16, 0, 0:PC], neg_max_parts[:, :, :].bitcast(f32).rearrange("t a p -> t (a p)"),
                                 ident[0:PC, 0:PC], start=True, stop=True).then_inc(nmT_done, 1)

            pe.wait_ge(w_loaded, 48)
            pe.wait_ge(ctx_begun, 16)
            k_project(0, 0, 0, score_ps[:, 0, :])
            k_project(0, 0, 1, score_ps[:, 1, :])
            pe.wait_ge(consts, 1)
            for r in range(NR):
                pe.wait_ge(xn_ready, r + 1)
                last = nc.tensor.matmul(misc_ps[:, RT * r:RT * r + RT], xn[:, r, :], ident[0:RT, 0:RT],
                                        start=True, stop=True)
            last.then_inc(xT_done, 1)
            pe.wait_ge(ctx_loaded[0], 16)
            k_project(0, 0, 2, score_ps[:, 2, :])
            pe.wait_ge(xT_saved, 1)
            for g in range(G):
                nc.tensor.matmul(q_banks[g][0:MR, 0:TOK], wq_sb[:, g, :], xnT[:, :], start=True, stop=True
                                 ).then_inc(q_done, 1)
            for n in range(-2, MN):
                if n == 0:
                    pe.wait_ge(q_low_saved, G)
                    pe.wait_ge(qx_ready, 1)
                if n >= 0 and keys_of(n) is not None:
                    part, groups = keys_of(n)
                    pe.wait_ge(kx_loaded[0][part][groups], MOVES)
                if n >= 0:
                    max_scores(0, 0, n)
                job, k = FIRST_JOBS.get(n, (None, 0))
                if job == "V":
                    if k:
                        pe.wait_ge(v_saved, k)
                    v_project(0, k)
                if job == "K":
                    if k == 0:
                        pe.wait_ge(ctx_loaded[1], 16)
                    pe.wait_ge(k_low_saved, k + 1)
                    k_project(1, 1, k, score_ps[:, k, :])
            transpose_max(3)
            pe.wait_ge(nm_rows, 2)
            pe.wait_ge(kx_ones, 1)
            pe.wait_ge(k_low_saved, 2 * NCH)
            scores(0, 0)
            scores(0, 1)

            def body(i, par, keys_next=True, next_batch=True):
                b = batch(i, par)
                i1, par1 = nxt(i, par, 1)

                def one_chunk(chunks):
                    if not chunks:
                        return
                    n = chunks.pop(0)
                    if n == 0:
                        pe.wait_ge(qx_ready, b + 2)
                    if n == NB - 1:
                        pe.wait_ge(den_taken, b + 1)
                    first = keys_of(n)
                    if first is not None:
                        moved, _ = counts(pe, MOVES * (i1 + 1), MN * (b + 1) + n - NB + 1 if n >= NB else 0)
                        pe.wait_ge(kx_loaded[par1][first[0]][first[1]], moved)
                    max_scores(b + 1, par1, n)

                for t in range(KT):
                    chunks = list(MAX_STEPS[t]) if next_batch else []
                    for h in range(2):
                        if h:
                            pe.wait_ge(exp_done, NHS * b + 2 * t + 1)
                        if t < KT - 1:
                            scores(par, 2 * t + 2 + h)
                        elif next_batch:
                            pe.wait_ge(nm_rows, 2 * (b + 1) + h + 1)
                            scores(par1, h)
                        one_chunk(chunks)
                    if not next_batch and t == TOKEN_STEPS[0]:
                        pe.wait_ge(wo_loaded, 16 * H)
                        pe.wait_ge(o_norm_ready, B - 1)
                        project_out(0, NR - 1)
                    if not next_batch and t == TOKEN_STEPS[1]:
                        transpose_tokens(0, NR - 1, NR)
                    job, n = JOBS.get(t, (None, None))
                    if job == "V" and next_batch:
                        if keys_next or n == 0:
                            pe.wait_ge(k_saved, 2 * (NCH * (b + 2) + n))
                        else:
                            pe.wait_ge(v_saved, 3 * (b + 1) + n)
                        v_project(par1, n)
                    if job == "K" and keys_next:
                        loaded, taken = counts(pe, 16 * (i + 2), 3 * (b + 1) + n + 1)
                        if n == 0:
                            pe.wait_ge(ctx_loaded[par], loaded)
                        pe.wait_ge(v_saved, taken)
                        if t < KT - 1:
                            k_project(b + 2, par, n, misc_ps)
                    one_chunk(chunks)
                    if next_batch and t == TR_STEP:
                        transpose_max(3 * (b + 2))
                    pe.wait_ge(exp_done, NHS * b + 2 * t + 2)
                    attend(par, t, 0)
                    last = attend(par, t, 1)
                    one_chunk(chunks)
                last.then_inc(pv_done, 1)
                if keys_next and JOBS.get(KT - 1, (None, 0))[0] == "K":
                    k_project(b + 2, par, NCH - 1, misc_ps)
                saved, taken = counts(pe, b + 1, MN * (b + 2))
                pe.wait_ge(o_saved, saved)
                if next_batch:
                    pe.wait_ge(max_taken, taken)
                nc.tensor.matmul(max_ps[:, 2, 0:2 * PC], den_sel[:, :], o_sb[:, :], start=True, stop=True
                                 ).then_inc(den_done, 1)

            def project_out(first, end):
                for r in range(first, end):
                    for n in range(4):
                        last = nc.tensor.matmul(token_banks[r][0:RT, :], o_norm[:, r, n, :, :].rearrange("p b c -> p (b c)"),
                                                wo_sb[:, n, :], start=(n == 0), stop=(n == 3))
                last.then_inc(wo_done, 1)

            def transpose_tokens(first, end, ready):
                for r in range(first, end):
                    pe.wait_ge(xn_ready, ready + r + 1)
                    last = nc.tensor.matmul(misc_ps[:, RT * r:RT * r + RT], xn[:, r, :], ident[0:RT, 0:RT],
                                            start=True, stop=True)
                last.then_inc(xT_done, 1)

            with pe.Fori(0, B // 2 - 1) as i:
                body(i, 0)
                body(i, 1)
            body(3, 0, keys_next=False)
            body(3, 1, keys_next=False, next_batch=False)

            pe.wait_ge(exp_done, NHS * B)
            pe.wait_ge(o_norm_ready, B + 1)
            project_out(NR - 1, NR)
            transpose_tokens(NR - 1, NR, NR)
            pe.wait_ge(xT_saved, 3)
            pe.wait_ge(ffn_loaded, 16 * (1 + 2 * E))
            for r in range(NR):
                nc.tensor.matmul(max_ps[0:RT, 0, E * r:E * r + E], xnT[:, RT * r:RT * r + RT], gw_sb[:, :],
                                 start=True, stop=True).then_inc(logits_done, 1)

            def product3(out, w_high, w_low, high, low, start=True, stop=True):
                nc.tensor.matmul(out, w_high, high, start=start, stop=False, skip_group_check=True)
                nc.tensor.matmul(out, w_high, low, start=False, stop=False, skip_group_check=True)
                return nc.tensor.matmul(out, w_low, high, start=False, stop=stop, skip_group_check=True)

            def parts(kind, par, j):
                return [weight_parts[:, kind, par, s, 128 * j:128 * j + 128] for s in range(2)]

            def gate(par, j):
                product3(gate_banks[j % 2][:, 0:TOK], *parts(GATE, par, j), x_high, x_low).then_inc(gate_done, 1)

            def spread_weight(e, par):
                pe.wait_ge(select_ready, e + 1)
                nc.tensor.matmul(max_ps[:, par, 0:TOK], expert_now[:, par, :], combT, start=True, stop=True
                                 ).then_inc(bc_done, 1)

            pe.wait_ge(x_split, 1)
            for n in range(2 * FT):
                if n == 2 * FT - 2:
                    pe.wait_ge(comb_ready, 1)
                    for r in range(NR):
                        last = nc.tensor.matmul(max_ps[0:16, 2, RT * r:RT * r + RT],
                                                comb_parts[:, r, :, :].bitcast(f32).rearrange("t a e -> t (a e)"),
                                                ident[0:RT, 0:RT], start=True, stop=True)
                    last.then_inc(combT_done, 1)
                if n % FT == 0:
                    pe.wait_ge(weights_low, n // FT + 1)
                if n >= 2:
                    pe.wait_ge(gelu_ready, n - 1)
                gate(n // FT, n % FT)
            pe.wait_ge(combT_saved, 1)
            spread_weight(0, 0)
            pe.wait_ge(zeros_ready, 1)
            nc.tensor.matmul(o_ps[:, 0:TOK], zeros, x_high, start=True, stop=False, skip_group_check=True)

            def expert(i, par, gates=True, more=True):
                e = batch(i, par)

                def up(j):
                    if j >= NB:
                        pe.wait_ge(hact_full, FT * e + j - NB + 1)
                    product3(up_banks[j % NB][:, 0:TOK], *parts(UP, par, j), x_expert_high[:, par, :],
                             x_expert_low[:, par, :]).then_inc(up_done, 1)

                def next_gate(j):
                    if gates:
                        pe.wait_ge(gelu_ready, FT * (e + 2) + j - 1)
                        gate(par, j)

                def down(j):
                    pe.wait_ge(hact_ready, FT * e + j + 1)
                    product3(o_ps[:, 0:TOK], *parts(DOWN, par, j), hact_parts[:, j, 0, :], hact_parts[:, j, 1, :],
                             start=False, stop=not more and j == FT - 1).then_inc(down_done, 1)

                made = 3 * e + 3 if more else 3 * E - 1
                tokens, made = counts(pe, e + 1, made)
                pe.wait_ge(xe_ready, tokens)
                pe.wait_ge(weights_low, made)
                for j in range(FT):
                    up(j)
                if gates:
                    pe.wait_ge(weights_low, 3 * e + 5)
                for j in range(FT):
                    next_gate(j)
                    if not gates and j == 0:
                        pe.wait_ge(weights_low, 3 * E - 2 * more)
                    down(j)
                    if more and j == 0:
                        spread_weight(e + 1, 1 - par)

            with pe.Fori(0, E // 2 - 1) as i:
                expert(i, 0)
                expert(i, 1)
            expert(E // 2 - 1, 0, gates=False)
            expert(E // 2 - 1, 1, gates=False, more=False)
            pe.wait_ge(y_saved, 1)
            for r in range(NR):
                nc.tensor.matmul(out_banks[r][0:RT, 0:D], yT[:, RT * r:RT * r + RT], ident[:, :],
                                 start=True, stop=True).then_inc(yT_done, 1)


JOBS = {0: ("V", 0), 2: ("K", 0), 4: ("V", 1), 6: ("K", 1), 9: ("V", 2), KT - 1: ("K", 2)}
MAX_STEPS = [[0, 1, 2], [3, 4], [5, 6, 7], [8, 9], [10, 11, 12], [13, 14, 15], [16, 17, 18], [19, 20, 21], [22, 23], [], [], []]
NM_STEP = 8
TOKEN_STEPS = [0, 8]
TR_STEP = 9
FIRST_WEIGHTS = [(0, 0), (0, 1), (1, 0), (2, 0), (0, 2)]
FIRST_SPLITS = [5, 8, 18]
FIRST_JOBS = {-2: ("V", 0), -1: ("K", 0), 1: ("V", 1), 5: ("K", 1), 9: ("V", 2), 13: ("K", 2)}


def kernel(x, ctx_1024, g_xattn, g_ffn, L0_xattn_w_q, L0_xattn_w_k, L0_xattn_w_v, L0_xattn_w_o,
           L0_ffn_gate_w, L0_ffn_gate_up_w, L0_ffn_down_w):
    import numpy as np
    import concourse.bacc as bacc
    from concourse.bass_utils import run_bass_kernel_spmd

    layout = np.ascontiguousarray
    arrays = {
        "x": layout(np.asarray(x).reshape(NR, RT, D).transpose(1, 0, 2)),
        "ctxT": layout(np.asarray(ctx_1024).transpose(0, 2, 1)),
        "g_attn": np.asarray(g_xattn),
        "g_ffn": np.asarray(g_ffn),
        "wqT": layout(np.tile(np.asarray(L0_xattn_w_q).T.reshape(D, G, 1, 32), (1, 1, 3, 1)).reshape(D, G, MR)),
        "wkT": layout(np.asarray(L0_xattn_w_k).T),
        "wvT": layout(np.asarray(L0_xattn_w_v).T),
        "woT": layout(np.asarray(L0_xattn_w_o).T),
        "gwT": layout(np.asarray(L0_ffn_gate_w).T),
        "guT": layout(np.asarray(L0_ffn_gate_up_w).transpose(2, 0, 1)),
        "dnT": layout(np.asarray(L0_ffn_down_w).reshape(E, D, FT, 128).transpose(3, 0, 2, 1)),
    }
    nc = bacc.Bacc("TRN2", target_bir_lowering=False, num_devices=1)
    f32 = mybir.dt.float32
    args = [nc.dram_tensor(f"in_{n}", a.shape, f32, kind="ExternalInput").ap() for n, a in arrays.items()]
    result = nc.dram_tensor("out_0", (RT, NR, D), f32, kind="ExternalOutput").ap()
    flamingo_block(nc, *args, result)
    ran = run_bass_kernel_spmd(nc, [{f"in_{n}": a for n, a in arrays.items()}], core_ids=[0])
    return ran.results[0]["out_0"].transpose(1, 0, 2).reshape(B, TQ, D)
```
